# Optimizing a Trainium2 kernel written in Bass

```python
import numpy as np
import jax
import jax.numpy as jnp

def _softmax(x, axis=-1):
    return jax.nn.softmax(x, axis=axis)

def _gelu(x):
    return jax.nn.gelu(x, approximate=True)

def _silu(x):
    return jax.nn.silu(x)

def _sigmoid(x):
    return jax.nn.sigmoid(x)

def _layernorm(x, axis=-1, eps=1e-05):
    m = jnp.mean(x, axis=axis, keepdims=True)
    v = jnp.var(x, axis=axis, keepdims=True)
    return (x - m) / jnp.sqrt(v + eps)

def _scatter_add(tgt, idx, src, axis=0):
    return tgt.at[idx].add(src)

def _segment_sum(src, seg, n):
    return jax.ops.segment_sum(src, seg, n)
kernel_name = 'mk_decoder_postln_d1_seqx_r4_de9041'

def setup_inputs(seed: int=0):
    np.random.seed(seed)
    _w = jnp.asarray

    def _rec_inputs():
        import jax
        import jax.numpy as jnp
        _rk = jax.random.key(seed)
        x = -0.0002928 + 1 * jax.random.normal(jax.random.fold_in(_rk, 1), (64, 128, 256), jnp.float32)
        _lenS = 128 - jax.random.randint(jax.random.fold_in(_rk, 7), (64,), 0, max(1, 128 // 4) + 1, jnp.int32)
        _lenS2 = 128 - jax.random.randint(jax.random.fold_in(_rk, 8), (64,), 0, max(1, 128 // 4) + 1, jnp.int32)
        _ctx_1024P = jax.random.normal(jax.random.fold_in(_rk, 11), (64, 16, 256), jnp.float32)
        _ctx_1024c = jax.random.dirichlet(jax.random.fold_in(_rk, 511), 0.3 * jnp.ones((16,), jnp.float32), (64, 128))
        _ctx_1024t = jnp.einsum('bsk,bkd->bsd', _ctx_1024c, _ctx_1024P)
        _ctx_1024t = _ctx_1024t * jax.lax.rsqrt(jnp.mean(jnp.square(_ctx_1024t)) + 1e-12) * 0.953939
        ctx_1024 = -1.39393e-06 + 0.999914 * (_ctx_1024t + 0.3 * jax.random.normal(jax.random.fold_in(_rk, 611), (64, 128, 256), jnp.float32))
        return (x, ctx_1024)
    x, ctx_1024 = _rec_inputs()

    def _L0_attn_setup():
        import jax, jax.numpy as jnp
        import numpy as np
        import math
        B, T, E, H, DQ, NB, MAXLEN = (4, 256, 256, 16, 64, 10, 256)
        NEG = -1000000000.0

        def _attn_forward(X, Wq, bq, Wk, Wv, Wproj, bproj, Wr, br, b_nd):
            b, t, e = X.shape
            maxlen = b_nd.shape[1]
            nb = b_nd.shape[0]
            h = H
            dq = Wq.shape[1] // h
            Q = (X @ Wq + bq).reshape(b, t, h, dq).transpose(0, 2, 1, 3)
            K = (X @ Wk).reshape(b, t, h, dq).transpose(0, 2, 1, 3)
            V = (X @ Wv).reshape(b, t, h, dq).transpose(0, 2, 1, 3)
            R = (X @ Wr + br).reshape(b, t, h, nb).transpose(0, 2, 1, 3)
            d = jnp.arange(t)[:, None] - jnp.arange(t)[None, :]
            valid = (d >= 0) & (d < maxlen)
            bias = jnp.where(valid, 0.0, NEG).astype(jnp.float32)
            D_ntT = jnp.where(valid[None, :, :], b_nd[:, jnp.clip(d, 0, maxlen - 1)], 0.0)
            extra = jnp.einsum('bhtn,ntp->bhtp', R, D_ntT)
            logits = jnp.einsum('bhtd,bhpd->bhtp', Q, K) / math.sqrt(dq) + bias + extra
            W = jax.nn.softmax(logits, axis=-1)
            A = jnp.einsum('bhtp,bhpd->bhtd', W, V)
            A = A.transpose(0, 2, 1, 3).reshape(b, t, h * dq)
            return A @ Wproj + bproj
        key = jax.random.key(seed)
        k = jax.random.split(key, 10)
        X = jax.random.normal(k[0], (B, T, E), jnp.float32)
        Wq = jax.random.normal(k[1], (E, H * DQ), jnp.float32) * (0.1 / math.sqrt(E))
        bq = jnp.zeros((H * DQ,), jnp.float32)
        Wk = jax.random.normal(k[2], (E, H * DQ), jnp.float32) * (0.2 / math.sqrt(E))
        Wv = jax.random.normal(k[3], (E, H * DQ), jnp.float32) * (1.0 / math.sqrt(E))
        Wproj = jax.random.normal(k[4], (H * DQ, E), jnp.float32) * (1.0 / math.sqrt(H * DQ))
        bproj = jnp.zeros((E,), jnp.float32)
        Wr = jax.random.normal(k[5], (E, H * NB), jnp.float32) * (0.1 / math.sqrt(E))
        br = jnp.zeros((H * NB,), jnp.float32)
        b_nd = jax.random.normal(k[6], (NB, MAXLEN), jnp.float32) * 0.2
        return dict(X=X, Wq=Wq, bq=bq, Wk=Wk, Wv=Wv, Wproj=Wproj, bproj=bproj, Wr=Wr, br=br, b_nd=b_nd)
    _L0_attn_all = _L0_attn_setup()
    _L0_attn_in = {k: v for k, v in _L0_attn_all.items() if k in ('Wq', 'bq', 'Wk', 'Wv', 'Wproj', 'bproj', 'Wr', 'br', 'b_nd')}
    del _L0_attn_all

    def _L0_xattn_setup():
        import jax, jax.numpy as jnp
        import numpy as np
        HEADS = 16
        NEG = -1000000000.0
        key = jax.random.key(seed)
        ks = jax.random.split(key, 7)
        B, T, C = (2, 512, 256)
        s = 1.0 / np.sqrt(C)
        return {'q': jax.random.normal(ks[0], (B, T, C), jnp.float32), 'k': jax.random.normal(ks[1], (B, T, C), jnp.float32), 'v': jax.random.normal(ks[2], (B, T, C), jnp.float32), 'Wq': jax.random.normal(ks[3], (C, C), jnp.float32) * s, 'Wk': jax.random.normal(ks[4], (C, C), jnp.float32) * s, 'Wv': jax.random.normal(ks[5], (C, C), jnp.float32) * s, 'Wo': jax.random.normal(ks[6], (C, C), jnp.float32) * s}
    _L0_xattn_all = _L0_xattn_setup()
    _L0_xattn_in = {k: v for k, v in _L0_xattn_all.items() if k in ('Wq', 'Wk', 'Wv', 'Wo')}
    del _L0_xattn_all

    def _L0_ffn_setup():
        import jax, jax.numpy as jnp
        import numpy as np
        E = 8
        TOP_K = 2
        H = 256
        I = 128
        B, S = (2, 512)

        def _moe_forward(hidden_states, w_gate, w_fc, w_proj):
            b, s, h = hidden_states.shape
            x = hidden_states.reshape(-1, h)
            T = x.shape[0]
            router_logits = x @ w_gate.T
            topk_vals, topk_idx = jax.lax.top_k(router_logits, TOP_K)
            router_weights = jax.nn.softmax(topk_vals.astype(jnp.float32), axis=-1).astype(x.dtype)
            gates = jnp.zeros((T, E), x.dtype).at[jnp.arange(T)[:, None], topk_idx].add(router_weights)
            hmid = jax.nn.gelu(jnp.einsum('th,eih->tei', x, w_fc), approximate=False)
            y = jnp.einsum('tei,ehi->teh', hmid, w_proj)
            out = jnp.einsum('teh,te->th', y, gates)
            return out.reshape(b, s, h)
        key = jax.random.key(seed)
        k0, k1, k2, k3 = jax.random.split(key, 4)
        std = 0.02
        return {'hidden_states': jax.random.normal(k0, (B, S, H), dtype=jnp.float32), 'w_gate': jax.random.normal(k1, (E, H), dtype=jnp.float32) * std, 'w_fc': jax.random.normal(k2, (E, I, H), dtype=jnp.float32) * std, 'w_proj': jax.random.normal(k3, (E, H, I), dtype=jnp.float32) * (std / np.sqrt(48.0))}
    _L0_ffn_all = _L0_ffn_setup()
    _L0_ffn_in = {k: v for k, v in _L0_ffn_all.items() if k in ('w_gate', 'w_fc', 'w_proj')}
    del _L0_ffn_all
    return {'x': x, 'ctx_1024': ctx_1024, 'L0_attn_Wq': _L0_attn_in['Wq'], 'L0_attn_bq': _L0_attn_in['bq'], 'L0_attn_Wk': _L0_attn_in['Wk'], 'L0_attn_Wv': _L0_attn_in['Wv'], 'L0_attn_Wproj': _L0_attn_in['Wproj'], 'L0_attn_bproj': _L0_attn_in['bproj'], 'L0_attn_Wr': _L0_attn_in['Wr'], 'L0_attn_br': _L0_attn_in['br'], 'L0_attn_b_nd': _L0_attn_in['b_nd'], 'L0_xattn_Wq': _L0_xattn_in['Wq'], 'L0_xattn_Wk': _L0_xattn_in['Wk'], 'L0_xattn_Wv': _L0_xattn_in['Wv'], 'L0_xattn_Wo': _L0_xattn_in['Wo'], 'L0_ffn_w_gate': _L0_ffn_in['w_gate'], 'L0_ffn_w_fc': _L0_ffn_in['w_fc'], 'L0_ffn_w_proj': _L0_ffn_in['w_proj']}

def reference(x, ctx_1024, L0_attn_Wq, L0_attn_bq, L0_attn_Wk, L0_attn_Wv, L0_attn_Wproj, L0_attn_bproj, L0_attn_Wr, L0_attn_br, L0_attn_b_nd, L0_xattn_Wq, L0_xattn_Wk, L0_xattn_Wv, L0_xattn_Wo, L0_ffn_w_gate, L0_ffn_w_fc, L0_ffn_w_proj):
    import jax
    import jax.numpy as jnp

    def _L0_attn_ref(X, Wq, bq, Wk, Wv, Wproj, bproj, Wr, br, b_nd):
        import jax, jax.numpy as jnp
        import numpy as np
        import math
        B, T, E, H, DQ, NB, MAXLEN = (4, 256, 256, 16, 64, 10, 256)
        NEG = -1000000000.0

        def _attn_forward(X, Wq, bq, Wk, Wv, Wproj, bproj, Wr, br, b_nd):
            b, t, e = X.shape
            maxlen = b_nd.shape[1]
            nb = b_nd.shape[0]
            h = H
            dq = Wq.shape[1] // h
            Q = (X @ Wq + bq).reshape(b, t, h, dq).transpose(0, 2, 1, 3)
            K = (X @ Wk).reshape(b, t, h, dq).transpose(0, 2, 1, 3)
            V = (X @ Wv).reshape(b, t, h, dq).transpose(0, 2, 1, 3)
            R = (X @ Wr + br).reshape(b, t, h, nb).transpose(0, 2, 1, 3)
            d = jnp.arange(t)[:, None] - jnp.arange(t)[None, :]
            valid = (d >= 0) & (d < maxlen)
            bias = jnp.where(valid, 0.0, NEG).astype(jnp.float32)
            D_ntT = jnp.where(valid[None, :, :], b_nd[:, jnp.clip(d, 0, maxlen - 1)], 0.0)
            extra = jnp.einsum('bhtn,ntp->bhtp', R, D_ntT)
            logits = jnp.einsum('bhtd,bhpd->bhtp', Q, K) / math.sqrt(dq) + bias + extra
            W = jax.nn.softmax(logits, axis=-1)
            A = jnp.einsum('bhtp,bhpd->bhtd', W, V)
            A = A.transpose(0, 2, 1, 3).reshape(b, t, h * dq)
            return A @ Wproj + bproj
        return _attn_forward(X, Wq, bq, Wk, Wv, Wproj, bproj, Wr, br, b_nd)

    def _L0_xattn_ref(q, k, v, Wq, Wk, Wv, Wo):
        import jax, jax.numpy as jnp
        import numpy as np
        HEADS = 16
        NEG = -1000000000.0
        B, T, C = q.shape
        h = HEADS
        dk = C // h

        def proj(x, W):
            return (x @ W.T).reshape(B, T, h, dk).transpose(0, 2, 1, 3)
        qh, kh, vh = (proj(q, Wq), proj(k, Wk), proj(v, Wv))
        scale = jnp.asarray(dk, q.dtype) ** 0.5
        scores = jnp.einsum('bhqd,bhkd->bhqk', qh / scale, kh)
        causal = jnp.tril(jnp.ones((T, T), dtype=bool))
        scores = jnp.where(causal[None, None], scores, jnp.asarray(NEG, scores.dtype))
        attn = jax.nn.softmax(scores, axis=-1)
        out = jnp.einsum('bhqk,bhkd->bhqd', attn, vh)
        concat = out.transpose(0, 2, 1, 3).reshape(B, T, C)
        return concat @ Wo.T

    def _L0_ffn_ref(hidden_states, w_gate, w_fc, w_proj):
        import jax, jax.numpy as jnp
        import numpy as np
        E = 8
        TOP_K = 2
        H = 256
        I = 128
        B, S = (2, 512)

        def _moe_forward(hidden_states, w_gate, w_fc, w_proj):
            b, s, h = hidden_states.shape
            x = hidden_states.reshape(-1, h)
            T = x.shape[0]
            router_logits = x @ w_gate.T
            topk_vals, topk_idx = jax.lax.top_k(router_logits, TOP_K)
            router_weights = jax.nn.softmax(topk_vals.astype(jnp.float32), axis=-1).astype(x.dtype)
            gates = jnp.zeros((T, E), x.dtype).at[jnp.arange(T)[:, None], topk_idx].add(router_weights)
            hmid = jax.nn.gelu(jnp.einsum('th,eih->tei', x, w_fc), approximate=False)
            y = jnp.einsum('tei,ehi->teh', hmid, w_proj)
            out = jnp.einsum('teh,te->th', y, gates)
            return out.reshape(b, s, h)
        return _moe_forward(hidden_states, w_gate, w_proj=w_proj, w_fc=w_fc)
    x = _layernorm(x + _L0_attn_ref(x, L0_attn_Wq, L0_attn_bq, L0_attn_Wk, L0_attn_Wv, L0_attn_Wproj, L0_attn_bproj, L0_attn_Wr, L0_attn_br, L0_attn_b_nd), axis=-1)
    x = _layernorm(x + _L0_xattn_ref(x, ctx_1024, ctx_1024, L0_xattn_Wq, L0_xattn_Wk, L0_xattn_Wv, L0_xattn_Wo), axis=-1)
    x = _layernorm(x + _L0_ffn_ref(x, L0_ffn_w_gate, L0_ffn_w_fc, L0_ffn_w_proj), axis=-1)
    return x

_drawn_inputs = setup_inputs


def setup_inputs(seed=0):
    import zlib

    import numpy as np

    out = dict(_drawn_inputs(seed))
    spreads = {'L0_attn_bq': (0.0, 0.8), 'L0_attn_bproj': (0.0, 0.1), 'L0_attn_br': (0.0, 0.8)}
    factors = {'L0_attn_Wq': 8.0,
     'L0_attn_Wk': 8.0,
     'L0_attn_Wr': 6.348,
     'L0_attn_b_nd': 4.462,
     'L0_ffn_w_gate': 8.0,
     'L0_ffn_w_fc': 8.0,
     'L0_ffn_w_proj': 8.0}
    for name, (base, spread) in spreads.items():
        noise = np.random.default_rng([zlib.crc32(name.encode()), seed]).standard_normal(out[name].shape)
        drawn = base * np.exp(spread * noise) if base else spread * noise
        out[name] = jnp.asarray(drawn.astype(out[name].dtype))
    for name, factor in factors.items():
        out[name] = (out[name] * factor).astype(out[name].dtype)
    return out
```

```python
from contextlib import ExitStack

import concourse.bass as bass
from concourse import mybir

F32 = mybir.dt.float32
F32R = mybir.dt.float32r
U32 = mybir.dt.uint32
ALU = mybir.AluOpType
ACT = mybir.ActivationFunctionType

P = 128
BIG = 1.0e9
EPS = 1e-5

FILL = [
    ([("VX", 0, -1), ("Q", 1, 0)], [("K", 1, 0)]),
    ([("V", 1, 0)], [("WO", 0, -2)]),
    ([("Q", 2, 0)], [("K", 2, 0), ("LN2", 0, -2)]),
    ([("X2T", 0, -2), ("V", 2, 0)], [("Q", 3, 0)]),
    ([("K", 3, 0), ("RT", 0, -2)], [("V", 3, 0)]),
    ([("GATE", 0, -2)], [("XS", 0, 1), ("GT", 0, -2)]),
    ([("R", 0, 1), ("R", 1, 1)], [("C", 0, 1), ("C", 1, 1), ("R", 2, 1)]),
    ([("C", 2, 1), ("C", 3, 1), ("R", 3, 1)], [("C", 4, 1), ("C", 5, 1)]),
    ([("C", 6, 1), ("C", 7, 1)], [("X1C", 0, -1)]),
    ([("CS", 0, 0), ("WP", 0, 0)], []),
    ([("FC", 0, -2), ("FC", 1, -2)], [("FC", 2, -2), ("FC", 3, -2), ("LN1", 0, 0)]),
    ([("GB", 0, -2)], [("X1T", 0, 0), ("GB", 1, -2)]),
    ([("MO", 0, -2)], [("Q", 0, 1)]),
    ([("GB", 2, -2), ("MO", 1, -2)], [("K", 0, 1)]),
    ([("GB", 3, -2), ("MO", 2, -2)], [("V", 0, 1), ("MO", 3, -2)]),
    ([("QX", 0, 0)], [("LN3", 0, -2), ("KX", 0, 0)]),
]
SLOTS = len(FILL)
BANKED = {"Q": 4, "K": 4, "V": 4, "R": 4, "C": 8, "WP": 1, "X1T": 1, "QX": 1, "KX": 1, "VX": 1,
          "WO": 1, "X2T": 1, "RT": 1, "GT": 1, "FC": 4, "GB": 4}
BANK_ORDER = [it for a, b in FILL for it in a + b if it[0] in BANKED]
BANK = {(w, n): j % 2 for j, (w, n, _) in enumerate(BANK_ORDER)}


def decoder_kernel(nc, x, x_t, ctx_t, wq, bq, wk, wv, wproj, bproj, wr, br, b_rev,
                   xwq_t, xwk_t, xwv_t, xwo_t, wg_t, wfc_t, wpj_t, consts, out):
    B, T, E = x.shape
    NG = B // 2
    HD = wq.shape[1]
    H = 16
    DQ = HD // H
    NB = b_rev.shape[0]
    NE, I = wfc_t.shape[1], wfc_t.shape[2]
    XD = E // H
    KC = E // P
    N2 = 2 * T
    RW = 4 * NB
    R3 = 3 * RW
    ROW = 4 * T + T
    assert T == P and E == 2 * P and DQ == 64 and XD == 16 and I == P and NE == 8 and R3 <= P

    scratch = nc.dram_tensor("bias_scratch", [8, T * ROW], F32, kind="Internal").ap()

    with ExitStack() as es:
        def sb(name, cols, dt=F32, parts=P):
            return es.enter_context(nc.sbuf_tensor(name, [parts, cols], dt))

        def ps(name):
            return es.enter_context(nc.psum_tensor(name, [P, 512], F32))

        def sem(name):
            return es.enter_context(nc.semaphore(name))

        def pair(name, cols):
            return sb(name + "_hi", cols, F32R), sb(name + "_lo", cols, F32R)

        wq_s, wk_s, wv_s = (pair(n, KC * HD) for n in ("wq_s", "wk_s", "wv_s"))
        xwq_s, xwk_s, xwv_s = (pair(n, KC * E) for n in ("xwq_s", "xwk_s", "xwv_s"))
        wr_s = pair("wr_s", KC * 4 * R3)
        wfc_s, wpj_s = pair("wfc_s", KC * NE * I), pair("wpj_s", NE * E)
        wg_s = pair("wg_s", KC * NE)
        wp_s = sb("wp_s", (HD // P) * E)
        wo_s = sb("wo_s", KC * E)
        bq_s = sb("bq_s", HD // P)
        br_s = sb("br_s", 4)
        bproj_s = sb("bproj_s", E)
        toep = sb("toep", 4 * T, F32R)
        const = sb("const", consts.shape[1])
        ident, cmask, xmask = const[:, 0:P], const[:, P:2 * P], const[:, 2 * P:3 * P]
        pick, halfpow, iota8 = const[:, 3 * P:3 * P + 6], const[:, 3 * P + 6:3 * P + 8], const[:, 3 * P + 8:3 * P + 16]
        one_r = sb("one_r", NE, F32R, NE)
        raw = sb("raw", KC * N2)
        xt = pair("xt", KC * N2)
        ct = pair("ct", KC * N2)
        qkv = sb("qkv", 2 * 1024)
        q_t, v_s = qkv[:, 0:1024], qkv[:, 1024:2048]
        k_t = [sb(f"k_t{j}", 1024) for j in range(2)]
        at = sb("at", 8 * N2)
        r_st = [sb(f"r_st{j}", N2, F32R) for j in range(2)]
        c_s = [sb(f"c_s{j}", 4 * T) for j in range(2)]
        bias = [sb(f"bias{j}", 4 * T) for j in range(4)]
        prob = [sb(f"prob{j}", 4 * T) for j in range(2)]
        prob_t = [sb(f"prob_t{j}", 4 * T) for j in range(2)]
        low = [sb(f"low{j}", 4) for j in range(2)]
        total = [sb(f"total{j}", 4) for j in range(2)]
        inv = [sb(f"inv{j}", 4) for j in range(2)]
        xn = sb("xn", 2 * E)
        y = sb("y", 2 * E)
        r_f = y[:, 0:N2]
        stat = sb("stat", 2 * 6)
        mv = sb("mv", 2 * 2)
        rstd = [sb(f"rstd{n}", 4) for n in (1, 2, 3)]
        x1 = sb("x1", 2 * E)
        x1_old = sb("x1_old", 2 * E)
        x1_t = pair("x1_t", KC * N2)
        qx = sb("qx", KC * N2)
        kx = [sb(f"kx{j}", KC * N2) for j in range(2)]
        vx = sb("vx", 2 * H * 2 * XD)
        ax = sb("ax", KC * N2)
        x2 = sb("x2", 2 * E)
        x2_t = pair("x2_t", KC * N2)
        logit = sb("logit", 2 * NE)
        top = sb("top", 2 * 8)
        topi = sb("topi", 2 * 8, U32)
        topf = sb("topf", 2 * 8)
        gsc = sb("gsc", 8)
        gate = sb("gate", 2 * NE)
        gate2 = sb("gate2", 2 * NE)
        g_t = (sb("g_t_hi", N2, F32R, NE), sb("g_t_lo", N2, F32R, NE))
        hg = pair("hg", 2 * N2)

        S = [ps("ps_s0"), ps("ps_s1")]
        TP = [ps("ps_t0"), ps("ps_t1")]
        AV = ps("ps_av")
        FB = [ps("ps_f0"), ps("ps_f1")]
        MOB = ps("ps_mo")

        pe = {w: sem(f"pe_{w}") for w in list(BANKED) + ["MO"]}
        ev = {w: sem(f"ev_{w}") for w in list(BANKED) + ["MO"]}
        scores = {h: sem(f"scores_{h}") for h in "AB"}
        masked = {h: sem(f"masked_{h}") for h in "AB"}
        exped = {h: sem(f"exped_{h}") for h in "AB"}
        inved = {h: sem(f"inved_{h}") for h in "AB"}
        normed = {h: sem(f"normed_{h}") for h in "AB"}
        turned = {h: sem(f"turned_{h}") for h in "AB"}
        prob_out = {h: sem(f"prob_out_{h}") for h in "AB"}
        summed = {h: sem(f"summed_{h}") for h in "AB"}
        av_out = {h: sem(f"av_out_{h}") for h in "AB"}
        x_split, x_split_lo = sem("x_split"), sem("x_split_lo")
        c_split, c_split_lo = sem("c_split"), sem("c_split_lo")
        r_rounded = sem("r_rounded")
        x1t_hi, x2t_hi = sem("x1t_hi"), sem("x2t_hi")
        xn_ready, x1_kept = sem("xn_ready"), sem("x1_kept")
        stats_ready = [sem(f"stats_ready{n}") for n in (1, 2, 3)]
        rstd_ready = [sem(f"rstd_ready{n}") for n in (1, 2, 3)]
        ln_done = [sem(f"ln_done{n}") for n in (1, 2, 3)]
        tops_ready, gexp_ready, gate_ready = sem("tops_ready"), sem("gexp_ready"), sem("gate_ready")
        gate_copied = sem("gate_copied")
        h_hi, h_lo = sem("h_hi"), sem("h_lo")
        ld_xt, ld_xn, ld_ct, st_out = sem("ld_xt"), sem("ld_xn"), sem("ld_ct"), sem("st_out")
        bias_w = [sem(f"bias_w{k}") for k in range(8)]
        bias_r = [sem(f"bias_r{k}") for k in range(8)]
        ld_w = [sem(f"ld_w{j}") for j in range(2)]
        w_hi, w_lo = sem("w_hi"), sem("w_lo")
        ld_c = [sem(f"ld_c{j}") for j in range(24)]
        const_pool, const_dve = sem("const_pool"), sem("const_dve")
        pad_w = sem("pad_w")
        dve_passed, pool_passed, sp_passed = sem("dve_passed"), sem("pool_passed"), sem("sp_passed")
        ev_rs = sem("ev_rs")
        rt_chain, ga_chain = sem("rt_chain"), sem("ga_chain")
        ln_chain = [sem(f"ln_chain{n}") for n in (1, 2, 3)]
        eps_added = [sem(f"eps_added{n}") for n in (1, 2, 3)]

        def live(g):
            return not isinstance(g, int) or 0 <= g < NG

        def need(eng, s, value):
            if not isinstance(value, int) or value > 0:
                eng.wait_ge(s, value)

        def passed(eng, mark):
            eng.sem_inc(mark, 1)

        def heads_at(i, k):
            if k >= SLOTS:
                i, k = i + 1, k - SLOTS
            if k < 0:
                i, k = i - 1, k + SLOTS
            g = i if k < 8 else i - 1
            return ("A" if k < 8 else "B", g, k % 8) if live(g) else None

        def heads_before(i, k, d):
            k -= d
            while True:
                got = heads_at(i, k)
                if got or not isinstance(i, int):
                    return got
                k -= 8
                if 16 * i + k < 0:
                    return None
                while k < 0:
                    i, k = i - 1, k + SLOTS

        def rounds(eng, one_round):
            for i in (-1, 0, 1, 2):
                one_round(i)
            with eng.Fori(3, NG - 1) as i:
                one_round(i)
            for i in (NG - 1, NG, NG + 1):
                one_round(i)

        wq_d = wq.rearrange("(k p) n -> p k n", p=P)
        wk_d = wk.rearrange("(k p) n -> p k n", p=P)
        wv_d = wv.rearrange("(k p) n -> p k n", p=P)
        split_w = [
            (wq_d, wq_s, KC * HD, -1.0 / 8.0),
            (wk_d, wk_s, KC * HD, 1.0),
            (wv_d, wv_s, KC * HD, 1.0),
            (wr, wr_s, KC * 4 * R3, 1.0),
            (xwq_t.rearrange("(k p) n -> p k n", p=P), xwq_s, KC * E, -1.0 / 4.0),
            (xwk_t.rearrange("(k p) n -> p k n", p=P), xwk_s, KC * E, 1.0),
            (xwv_t.rearrange("(k p) n -> p k n", p=P), xwv_s, KC * E, 1.0),
            (wfc_t.rearrange("(k p) e i -> p k (e i)", p=P), wfc_s, KC * NE * I, 1.0),
            (wpj_t.rearrange("p e n -> p (e n)"), wpj_s, NE * E, 1.0),
            (wg_t.rearrange("(k p) n -> p k n", p=P), wg_s, KC * NE, 1.0),
        ]
        stages = [at[:, 0:2048], qkv[:, 0:2048]]
        NW = len(split_w)

        x_g = x.rearrange("(g s) t e -> g t s e", s=2)
        out_g = out.rearrange("(g s) t e -> g t s e", s=2)
        xt_g = x_t.rearrange("(k p) (g n) -> g p k n", p=P, n=N2)
        ct_g = ctx_t.rearrange("(k p) (g n) -> g p k n", p=P, n=N2)

        block = es.enter_context(nc.Block())

        @block.sync
        def _(sp):
            for n, (src, _, cols, _) in enumerate(split_w):
                if n >= 2:
                    sp.wait_ge(w_lo, n - 1)
                if src is wr:
                    for d in range(3):
                        for k in range(KC):
                            dst = stages[n % 2][:, k * 4 * R3:(k + 1) * 4 * R3].rearrange("p (b d n) -> p b d n", b=4, d=3)
                            sp.dma_start(dst[:, :, d, :], wr[k * P:(k + 1) * P, :].rearrange("p (b n) -> p b n", b=4)
                                         ).then_inc(ld_w[n % 2], 16)
                else:
                    dst = stages[n % 2][:, 0:cols]
                    if len(src.shape) == 3:
                        dst = dst.rearrange("p (k n) -> p k n", k=KC)
                    sp.dma_start(dst, src).then_inc(ld_w[n % 2], 16)
                if n == 0:
                    sp.dma_start(const[:, :], consts[:, :]).then_inc(ld_c[19], 16)
                    sp.dma_start(wp_s[:, :].rearrange("p (c n) -> p c n", n=E),
                                 wproj.rearrange("(c p) n -> p c n", p=P)).then_inc(ld_c[0], 16)
                    sp.dma_start(wo_s[:, :].rearrange("p (c n) -> p c n", n=E),
                                 xwo_t.rearrange("(c p) n -> p c n", p=P)).then_inc(ld_c[1], 16)
                    sp.dma_start(bq_s[:, :], bq[:, :]).then_inc(ld_c[2], 16)
                    sp.dma_start(bproj_s[:, :], bproj.rearrange("(a n) -> a n", a=1).to_broadcast([P, E])).then_inc(ld_c[3], 16)
                    for d in range(3):
                        sp.dma_start(br_s[d * RW:(d + 1) * RW, :], br[:, :]).then_inc(ld_c[4 + d], 16)
                    sp.wait_ge(const_pool, 3)
                    for d in range(3):
                        for h in range(4):
                            sp.dma_start(c_s[0][d * RW + h * NB:d * RW + (h + 1) * NB, h * T:(h + 1) * T],
                                         b_rev[:, :]).then_inc(ld_c[7 + 4 * d + h], 16)
                    for k in range(8):
                        sp.dma_start(scratch[k, :].rearrange("(t w) -> t w", w=ROW)[:, 4 * T:ROW],
                                     c_s[1][:, 0:T]).then_inc(pad_w, 16)

            def one_round(i):
                for k in range(SLOTS):
                    if k == 0 and live(i):
                        need(sp, ev["WP"], i)
                        sp.dma_start(xn[:, :].rearrange("p (s e) -> p s e", s=2), x_g[i]).then_inc(ld_xn, 16)
                    if k == 0 and live(i + 1):
                        need(sp, c_split, i)
                        need(sp, c_split_lo, i)
                        sp.dma_start(raw[:, :].rearrange("p (k n) -> p k n", k=KC), xt_g[i + 1]).then_inc(ld_xt, 16)
                    if k == 6 and live(i):
                        need(sp, x_split, i + 2 if live(i + 1) else NG)
                        need(sp, x_split_lo, i + 2 if live(i + 1) else NG)
                        sp.dma_start(raw[:, :].rearrange("p (k n) -> p k n", k=KC), ct_g[i]).then_inc(ld_ct, 16)
                    for what, n, off in FILL[k][0] + FILL[k][1]:
                        if what == "C" and live(i + off):
                            need(sp, ev["C"], 8 * (i + off) + n + 1)
                            passed(sp, sp_passed)
                            need(sp, bias_r[n], 16 * (i + off))
                            if isinstance(i, int) and i + off == 0 and n == 0:
                                sp.wait_ge(pad_w, 128)
                            sp.dma_start(scratch[n, :].rearrange("(t w) -> t w", w=ROW)[:, 0:4 * T],
                                         c_s[n % 2][:, :]).then_inc(bias_w[n], 16)
                    g, m = (i, k + 4) if k < 4 else (i + 1, k - 12)
                    if (k < 4 or k >= 12) and live(g):
                        sp.wait_ge(bias_w[m], 16 * (g + 1))
                        passed(sp, sp_passed)
                        need(sp, masked["A"], 32 * g + 4 * (m - 4) + 4)
                        sp.dma_start(bias[m % 4][:, :],
                                     scratch[m, T - 1:T - 1 + T * (ROW - 1)].rearrange("(t w) -> t w", w=ROW - 1)[:, 0:4 * T]
                                     ).then_inc(bias_r[m], 16)
                    if k == 15 and live(i - 2):
                        need(sp, ln_done[2], i - 1)
                        sp.dma_start(out_g[i - 2], x2[:, :].rearrange("p (s e) -> p s e", s=2)).then_inc(st_out, 16)

            rounds(sp, one_round)
            sp.wait_ge(st_out, 16 * NG)

        @block.tensor
        def _(te):
            te.wait_ge(w_lo, NW)
            te.wait_ge(const_dve, 6)
            te.wait_ge(const_pool, 5)
            te.wait_ge(ld_c[19], 16)
            te.wait_ge(ld_c[0], 16)
            te.wait_ge(ld_c[1], 16)
            users = [None, None]

            def free_bank(i, what, n):
                b = BANK[(what, n)]
                if users[b] is not None:
                    w, m, g = users[b]
                    need(te, ev[w], BANKED[w] * g + m + 1)
                return FB[b]

            def three(out_ap, stationary, moving, first, last):
                nc.tensor.matmul(out_ap, stationary(0), moving(0), start=first, stop=False)
                nc.tensor.matmul(out_ap, stationary(0), moving(1), start=False, stop=False)
                return nc.tensor.matmul(out_ap, stationary(1), moving(0), start=False, stop=last)

            def k3(t, k, n):
                return t[:, k * n:(k + 1) * n]

            def item(i, what, n, off):
                g = i + off
                if not live(g):
                    return
                if what == "MO":
                    te.wait_ge(h_hi, 4 * g + n + 1)
                    te.wait_ge(h_lo, 4 * g + n + 1)
                    if n == 0:
                        need(te, ev["MO"], g)
                    for e in range(2):
                        for s in range(2):
                            for a, b in ((0, 0), (0, 1), (1, 0)):
                                last = nc.tensor.matmul(
                                    MOB[:, s * E:(s + 1) * E], hg[a][:, e * N2 + s * T:e * N2 + (s + 1) * T],
                                    k3(wpj_s[b], 2 * n + e, E), start=(n == 0 and e == 0 and s == 0 and a == 0 and b == 0),
                                    stop=(n == 3 and e == 1 and a == 1), skip_group_check=True)
                    last.then_inc(pe["MO"], 1)
                    return
                if what not in BANKED:
                    return
                F = free_bank(i, what, n)
                if what in "QK":
                    if n == 0:
                        te.wait_ge(x_split_lo, g + 1)
                    w = wq_s if what == "Q" else wk_s
                    for j in range(2):
                        c = 2 * n + j
                        for k in range(KC):
                            last = three(F[:, j * N2:(j + 1) * N2],
                                         lambda a: w[a][:, k * HD + c * P:k * HD + (c + 1) * P],
                                         lambda a: k3(xt[a], k, N2), k == 0, k == KC - 1)
                elif what == "V":
                    for s in range(2):
                        for k in range(KC):
                            last = three(F[:, s * 256:(s + 1) * 256],
                                         lambda a: xt[a][:, k * N2 + s * T:k * N2 + (s + 1) * T],
                                         lambda a: wv_s[a][:, k * HD + n * 256:k * HD + (n + 1) * 256], k == 0, k == KC - 1)
                elif what == "R":
                    te.wait_ge(x_split_lo, g + 1)
                    for k in range(KC):
                        last = three(F[0:R3, 0:N2],
                                     lambda a: wr_s[a][:, (k * 4 + n) * R3:(k * 4 + n + 1) * R3],
                                     lambda a: k3(xt[a], k, N2), k == 0, k == KC - 1)
                elif what == "C":
                    hb, s = n // 2, n % 2
                    te.wait_ge(ev_rs, 4 * g + hb + 1)
                    last = nc.tensor.matmul(F[:, :], r_st[hb % 2][0:R3, s * T:(s + 1) * T], toep[0:R3, :],
                                            start=True, stop=True)
                elif what == "WP":
                    te.wait_ge(av_out["A"], 8 * g + 8)
                    for s in range(2):
                        for c in range(8):
                            last = nc.tensor.matmul(F[:, s * E:(s + 1) * E], at[:, c * N2 + s * T:c * N2 + (s + 1) * T],
                                                    k3(wp_s, c, E), start=c == 0, stop=c == 7)
                elif what in ("X1T", "X2T"):
                    src, done = (x1, ln_done[0]) if what == "X1T" else (x2, ln_done[1])
                    te.wait_ge(done, g + 1)
                    for k in range(KC):
                        for s in range(2):
                            last = nc.tensor.transpose(F[:, k * N2 + s * T:k * N2 + (s + 1) * T],
                                                       src[:, s * E + k * P:s * E + (k + 1) * P], ident[:, :])
                elif what in ("QX", "KX"):
                    if what == "QX":
                        te.wait_ge(ev["X1T"], g + 1)
                    else:
                        te.wait_ge(c_split_lo, g + 1)
                    w, mov = (xwq_s, x1_t) if what == "QX" else (xwk_s, ct)
                    for c in range(KC):
                        for k in range(KC):
                            last = three(F[:, c * N2:(c + 1) * N2],
                                         lambda a: w[a][:, k * E + c * P:k * E + (c + 1) * P],
                                         lambda a: k3(mov[a], k, N2), k == 0, k == KC - 1)
                elif what == "VX":
                    te.wait_ge(c_split_lo, g + 1)
                    for s in range(2):
                        for k in range(KC):
                            last = three(F[:, s * E:(s + 1) * E],
                                         lambda a: ct[a][:, k * N2 + s * T:k * N2 + (s + 1) * T],
                                         lambda a: k3(xwv_s[a], k, E), k == 0, k == KC - 1)
                elif what == "WO":
                    te.wait_ge(av_out["B"], 8 * g + 8)
                    for s in range(2):
                        for c in range(KC):
                            last = nc.tensor.matmul(F[:, s * E:(s + 1) * E], ax[:, c * N2 + s * T:c * N2 + (s + 1) * T],
                                                    k3(wo_s, c, E), start=c == 0, stop=c == KC - 1)
                elif what == "RT":
                    te.wait_ge(ev["X2T"], g + 1)
                    for s in range(2):
                        for k in range(KC):
                            last = three(F[:, s * NE:(s + 1) * NE],
                                         lambda a: x2_t[a][:, k * N2 + s * T:k * N2 + (s + 1) * T],
                                         lambda a: k3(wg_s[a], k, NE), k == 0, k == KC - 1)
                elif what == "GT":
                    te.wait_ge(gate_ready, g + 1)
                    for s in range(2):
                        last = nc.tensor.transpose(F[0:NE, s * T:(s + 1) * T], gate[:, s * NE:(s + 1) * NE], ident[:, :])
                elif what == "GB":
                    te.wait_ge(ev["GT"], g + 1)
                    for e in range(2):
                        nc.tensor.matmul(F[:, e * N2:(e + 1) * N2], one_r[:, 2 * n + e:2 * n + e + 1].to_broadcast([NE, P]), g_t[0][:, :], start=True, stop=False)
                        last = nc.tensor.matmul(F[:, e * N2:(e + 1) * N2], one_r[:, 2 * n + e:2 * n + e + 1].to_broadcast([NE, P]), g_t[1][:, :],
                                                start=False, stop=True)
                elif what == "FC":
                    for e in range(2):
                        for k in range(KC):
                            last = three(F[:, e * N2:(e + 1) * N2],
                                         lambda a: wfc_s[a][:, k * NE * I + (2 * n + e) * I:k * NE * I + (2 * n + e + 1) * I],
                                         lambda a: k3(x2_t[a], k, N2), k == 0, k == KC - 1)
                last.then_inc(pe[what], 1)
                users[BANK[(what, n)]] = (what, n, g)

            def score(i, k):
                got = heads_at(i, k)
                if got is None:
                    return
                kind, g, m = got
                hb, s = m // 2, m % 2
                back = heads_before(i, k, 2)
                if back:
                    need(te, masked[back[0]], 32 * back[1] + 4 * back[2] + 4)
                if kind == "A":
                    te.wait_ge(ev["Q"], 4 * g + hb + 1)
                    te.wait_ge(ev["K"], 4 * g + hb + 1)
                else:
                    te.wait_ge(ev["QX"], g + 1)
                    te.wait_ge(ev["KX"], g + 1)
                for h in range(4):
                    if kind == "A":
                        col = (hb % 2) * 512 + (h // 2) * N2 + s * T
                        lhs, rhs = q_t[:, col:col + T], k_t[h % 2][:, col:col + T]
                    else:
                        r = 32 * hb
                        col = (h // 2) * N2 + s * T
                        lhs, rhs = qx[r:r + 32, col:col + T], kx[h % 2][r:r + 32, col:col + T]
                    last = nc.tensor.matmul(S[k % 2][:, h * T:(h + 1) * T], lhs, rhs, start=True, stop=True)
                last.then_inc(scores[kind], 1)

            def turn(i, k):
                got = heads_at(i, k)
                if got is None:
                    return
                kind, g, m = got
                te.wait_ge(normed[kind], 8 * g + m + 1)
                back = heads_before(i, k, 2)
                if back:
                    need(te, prob_out[back[0]], 8 * back[1] + back[2] + 1)
                for h in range(4):
                    last = nc.tensor.transpose(TP[k % 2][:, h * T:(h + 1) * T], prob[k % 2][:, h * T:(h + 1) * T], ident[:, :])
                last.then_inc(turned[kind], 1)

            def weigh(i, k):
                got = heads_at(i, k)
                if got is None:
                    return
                kind, g, m = got
                hb, s = m // 2, m % 2
                te.wait_ge(prob_out[kind], 8 * g + m + 1)
                back = heads_before(i, k, 1)
                if back:
                    need(te, av_out[back[0]], 8 * back[1] + back[2] + 1)
                if kind == "A":
                    te.wait_ge(ev["V"], 4 * g + hb + 1)
                else:
                    te.wait_ge(ev["VX"], g + 1)
                for h in range(4):
                    rhs = prob_t[k % 2][:, h * T:(h + 1) * T]
                    if kind == "A":
                        col = (hb % 2) * 512 + s * 256 + h * DQ
                        last = nc.tensor.matmul(AV[64 * (h % 2):64 * (h % 2) + 64, (h // 2) * T:(h // 2 + 1) * T],
                                                v_s[:, col:col + DQ], rhs, start=True, stop=True)
                    else:
                        c = h // 2
                        col = s * H * 32 + (8 * c + 2 * hb + h % 2) * 32
                        last = nc.tensor.matmul(AV[32 * hb:32 * hb + 32, c * T:(c + 1) * T], vx[:, col:col + 32], rhs,
                                                start=h % 2 == 0, stop=h % 2 == 1)
                last.then_inc(summed[kind], 1)

            def one_round(i):
                if not isinstance(i, int):
                    for what, n, off in BANK_ORDER[-2:]:
                        users[BANK[(what, n)]] = (what, n, i - 1 + off)
                for k in range(SLOTS):
                    score(i, k + 1)
                    for it in FILL[k][0]:
                        item(i, *it)
                    turn(i, k)
                    for it in FILL[k][1]:
                        item(i, *it)
                    weigh(i, k)
                if not isinstance(i, int):
                    for what, n, off in BANK_ORDER[-2:]:
                        users[BANK[(what, n)]] = (what, n, NG - 2 + off)

            rounds(te, one_round)

        @block.scalar
        def _(act):
            for n, (src, dst, cols, f) in enumerate(split_w):
                act.wait_ge(ld_w[n % 2], 16 * sum(3 * KC if split_w[j][0] is wr else 1 for j in range(n % 2, n + 1, 2)))
                nc.scalar.activation(dst[0][:, 0:cols], stages[n % 2][:, 0:cols], ACT.Copy, scale=f).then_inc(w_hi, 1)
            act.wait_ge(const_dve, 6)
            for j in range(3):
                act.wait_ge(ld_c[4 + j], 16)
            act.wait_ge(const_pool, 5)
            act.wait_ge(w_lo, NW)

            def item(i, what, n, off):
                g = i + off
                if not live(g):
                    return
                F = FB[BANK[(what, n)]] if what in BANKED else None
                if what == "Q":
                    act.wait_ge(pe["Q"], 4 * g + n + 1)
                    need(act, scores["A"], 8 * g + 2 * (n - 2) + 2)
                    for j in range(2):
                        last = nc.scalar.activation(q_t[:, (n % 2) * 512 + j * N2:(n % 2) * 512 + (j + 1) * N2],
                                                    F[:, j * N2:(j + 1) * N2], ACT.Identity,
                                                    bias=bq_s[:, 2 * n + j:2 * n + j + 1])
                    last.then_inc(ev["Q"], 1)
                elif what == "K":
                    act.wait_ge(pe["K"], 4 * g + n + 1)
                    need(act, scores["A"], 8 * g + 2 * (n - 2) + 2)
                    for j in range(2):
                        last = nc.scalar.activation(k_t[j][64 * j:64 * j + 64, (n % 2) * 512:(n % 2 + 1) * 512],
                                                    F[64 * j:64 * j + 64, :], ACT.Copy)
                    last.then_inc(ev["K"], 1)
                elif what == "V":
                    act.wait_ge(pe["V"], 4 * g + n + 1)
                    need(act, summed["A"], 8 * g + 2 * (n - 2) + 2)
                    nc.scalar.activation(v_s[:, (n % 2) * 512:(n % 2 + 1) * 512], F[:, :], ACT.Copy).then_inc(ev["V"], 1)
                elif what == "R":
                    act.wait_ge(pe["R"], 4 * g + n + 1)
                    need(act, ev_rs, 4 * g + n)
                    nc.scalar.activation(r_f[0:R3, :], F[0:R3, 0:N2], ACT.Identity,
                                         bias=br_s[0:R3, n:n + 1]).then_inc(ev["R"], 1)
                elif what in ("X1T", "X2T"):
                    t, s, last = (x1_t, x1t_hi, pe["QX"]) if what == "X1T" else (x2_t, x2t_hi, pe["FC"])
                    act.wait_ge(pe[what], g + 1)
                    need(act, last, g if what == "X1T" else 4 * g)
                    nc.scalar.activation(t[0][:, :], F[:, :], ACT.Copy).then_inc(s, 1)
                elif what == "QX":
                    act.wait_ge(pe["QX"], g + 1)
                    need(act, scores["B"], 8 * g)
                    nc.scalar.activation(qx[:, :], F[:, :], ACT.Copy).then_inc(ev["QX"], 1)
                elif what == "GATE":
                    act.wait_ge(tops_ready, g + 1)
                    nc.scalar.activation(gsc[:, 2:4], gsc[:, 0:2], ACT.Exp).then_inc(gexp_ready, 1)
                elif what == "FC":
                    act.wait_ge(pe["FC"], 4 * g + n + 1)
                    need(act, pe["WP"], (i + 1) if live(i) else NG)
                    nc.scalar.activation(at[:, n * 512:(n + 1) * 512], F[:, :], ACT.Gelu).then_inc(ev["FC"], 1)

            def exps(i, k):
                got = heads_at(i, k)
                if got is None:
                    return
                kind, g, m = got
                p = prob[k % 2]
                for h in range(4):
                    act.wait_ge(masked[kind], 32 * g + 4 * m + h + 1)
                    nc.scalar.activation(p[:, h * T:(h + 1) * T], p[:, h * T:(h + 1) * T], ACT.Exp,
                                         bias=low[k % 2][:, h:h + 1], scale=-1.0,
                                         accum_out=total[k % 2][:, h:h + 1]).then_inc(exped[kind], 1)

            def av(i, k):
                got = heads_at(i, k)
                if got is None:
                    return
                kind, g, m = got
                hb, s = m // 2, m % 2
                act.wait_ge(summed[kind], 8 * g + m + 1)
                if kind == "A":
                    if m == 0:
                        need(act, pe["WP"], g)
                        need(act, h_lo, 4 * (g - 2))
                    dst = at[:, :].rearrange("p (c s t) -> p c s t", c=8, s=2)[:, 2 * hb:2 * hb + 2, s, :]
                    nc.scalar.activation(dst, AV[:, 0:2 * T].rearrange("p (c t) -> p c t", c=2), ACT.Copy).then_inc(av_out["A"], 1)
                else:
                    if m == 0:
                        need(act, pe["WO"], g)
                    r = 32 * hb
                    dst = ax[r:r + 32, :].rearrange("p (c s t) -> p c s t", c=2, s=2)[:, :, s, :]
                    nc.scalar.activation(dst, AV[r:r + 32, 0:2 * T].rearrange("p (c t) -> p c t", c=2), ACT.Copy).then_inc(av_out["B"], 1)

            def one_round(i):
                for k in range(SLOTS):
                    exps(i, k + 1)
                    for it in FILL[k][0] + FILL[k][1]:
                        item(i, *it)
                    av(i, k)

            rounds(act, one_round)

        @block.vector
        def _(dve):
            for n, (src, dst, cols, f) in enumerate(split_w):
                dve.wait_ge(w_hi, n + 1)
                nc.vector.scalar_tensor_tensor(out=dst[1][:, 0:cols], in0=stages[n % 2][:, 0:cols], scalar=f,
                                               in1=dst[0][:, 0:cols].bitcast(F32), op0=ALU.mult,
                                               op1=ALU.subtract).then_inc(w_lo, 1)
            dve.wait_ge(ld_c[2], 16)
            nc.vector.tensor_scalar(bq_s[:, :], bq_s[:, :], -1.0 / 8.0, None, ALU.mult).then_inc(const_dve, 1)
            for j in range(12):
                dve.wait_ge(ld_c[7 + j], 16)
            dve.wait_ge(ld_c[19], 16)
            nc.vector.tensor_scalar(c_s[0][:, :], c_s[0][:, :], -1.0, None, ALU.mult).then_inc(const_dve, 1)
            dve.wait_ge(const_dve, 2)
            nc.vector.tensor_copy(toep[:, :], c_s[0][:, :]).then_inc(const_dve, 1)
            dve.wait_ge(const_dve, 3)
            nc.vector.tensor_scalar(y[:, :], toep[:, :].bitcast(F32), pick[:, 4:5], None, ALU.mult).then_inc(const_dve, 1)
            dve.wait_ge(const_dve, 4)
            nc.vector.scalar_tensor_tensor(out=toep[:, :], in0=c_s[0][:, :], scalar=pick[:, 5:6], in1=y[:, :],
                                           op0=ALU.mult, op1=ALU.add).then_inc(const_dve, 1)
            nc.vector.tensor_copy(one_r[:, :], ident[0:NE, 0:NE]).then_inc(const_dve, 1)
            dve.wait_ge(const_dve, 6)
            dve.wait_ge(pad_w, 128)

            def norm_stats(F, res, g, which, n_sem):
                ch = ln_chain[which]
                nc.vector.tensor_tensor(y[:, :], F, res, ALU.add).then_inc(n_sem, 1)
                dve.wait_ge(n_sem, g + 1)
                for s in range(2):
                    nc.vector.bn_stats(stat[:, 6 * s:6 * s + 6], y[:, s * E:(s + 1) * E]).then_inc(ch, 1)
                dve.wait_ge(ch, 2 * g + 2)
                passed(dve, dve_passed)
                for s in range(2):
                    nc.vector.bn_aggr(mv[:, 2 * s:2 * s + 2], stat[:, 6 * s:6 * s + 6]).then_inc(stats_ready[which], 1)

            def norm_apply(dst, g, which):
                dve.wait_ge(rstd_ready[which], g + 1)
                for s in range(2):
                    last = nc.vector.tensor_scalar(dst[:, s * E:(s + 1) * E], y[:, s * E:(s + 1) * E],
                                                   mv[:, 2 * s:2 * s + 1], rstd[which][:, 2 + s:3 + s], ALU.subtract, ALU.mult)
                last.then_inc(ln_done[which], 1)

            def item(i, what, n, off):
                g = i + off
                if not live(g):
                    return
                F = FB[BANK[(what, n)]] if what in BANKED else None
                if what == "XS":
                    dve.wait_ge(ld_xt, 16 * (g + 1))
                    need(dve, pe["V"], 4 * g)
                    nc.vector.tensor_copy(xt[0][:, :], raw[:, :]).then_inc(x_split, 1)
                elif what == "CS":
                    dve.wait_ge(ld_ct, 16 * (g + 1))
                    need(dve, pe["VX"], g)
                    nc.vector.tensor_copy(ct[0][:, :], raw[:, :]).then_inc(c_split, 1)
                elif what == "R":
                    dve.wait_ge(ev["R"], 4 * g + n + 1)
                    need(dve, pe["C"], 8 * g + 2 * (n - 2) + 2)
                    r = r_st[n % 2][0:R3, :]
                    nc.vector.tensor_scalar(r, r_f[0:R3, :], pick[0:R3, 2:3], None, ALU.mult).then_inc(r_rounded, 1)
                    dve.wait_ge(r_rounded, 4 * g + n + 1)
                    nc.vector.scalar_tensor_tensor(out=r, in0=r_f[0:R3, :], scalar=pick[0:R3, 3:4], in1=r.bitcast(F32),
                                                   op0=ALU.mult, op1=ALU.add).then_inc(ev_rs, 1)
                elif what == "C":
                    dve.wait_ge(pe["C"], 8 * g + n + 1)
                    if n >= 2:
                        dve.wait_ge(bias_w[n - 2], 16 * (g + 1))
                    else:
                        need(dve, bias_w[n + 6], 16 * g)
                    nc.vector.tensor_tensor(c_s[n % 2][:, :].rearrange("p (h t) -> p h t", h=4),
                                            F[:, :].rearrange("p (h t) -> p h t", h=4),
                                            cmask[:, :].unsqueeze(1).to_broadcast([P, 4, T]), ALU.add).then_inc(ev["C"], 1)
                elif what == "WP":
                    dve.wait_ge(pe["WP"], g + 1)
                    dve.wait_ge(xn_ready, g + 1)
                    need(dve, ln_done[1], g - 1)
                    need(dve, ev_rs, 4 * (i + 2 if live(i + 1) else NG))
                    norm_stats(F[:, :], xn[:, :], g, 0, ev["WP"])
                elif what == "LN1":
                    need(dve, x1_kept, g)
                    need(dve, pe["X1T"], g)
                    norm_apply(x1, g, 0)
                elif what in ("X1T", "X2T"):
                    t, s = (x1_t, x1t_hi) if what == "X1T" else (x2_t, x2t_hi)
                    dve.wait_ge(s, g + 1)
                    nc.vector.tensor_tensor(t[1][:, :], F[:, :], t[0][:, :].bitcast(F32), ALU.subtract).then_inc(ev[what], 1)
                elif what == "KX":
                    dve.wait_ge(pe["KX"], g + 1)
                    need(dve, scores["B"], 8 * g)
                    for j in range(2):
                        last = nc.vector.tensor_scalar(kx[j][:, :], F[:, :], pick[:, j:j + 1], None, ALU.mult)
                    last.then_inc(ev["KX"], 1)
                elif what == "VX":
                    dve.wait_ge(pe["VX"], g + 1)
                    need(dve, summed["B"], 8 * g)
                    for s in range(2):
                        dst = vx[:, s * 512:(s + 1) * 512].rearrange("p (h a d) -> p h a d", a=4, d=XD)[:, :, 0:4:3, :]
                        last = nc.vector.tensor_copy(dst, F[:, s * E:(s + 1) * E].rearrange("p (h a d) -> p h a d", a=2, d=XD))
                    last.then_inc(ev["VX"], 1)
                elif what == "WO":
                    dve.wait_ge(pe["WO"], g + 1)
                    dve.wait_ge(x1_kept, g + 1)
                    need(dve, ln_done[2], g)
                    norm_stats(F[:, :], x1_old[:, :], g, 1, ev["WO"])
                elif what == "LN2":
                    need(dve, st_out, 16 * g)
                    norm_apply(x2, g, 1)
                elif what == "RT":
                    dve.wait_ge(pe["RT"], g + 1)
                    nc.vector.tensor_copy(logit[:, :], F[:, 0:2 * NE]).then_inc(ev["RT"], 1)
                    dve.wait_ge(ev["RT"], g + 1)
                    passed(dve, dve_passed)
                    for s in range(2):
                        nc.vector.max(top[:, 8 * s:8 * s + 8], logit[:, NE * s:NE * s + NE]).then_inc(rt_chain, 1)
                    dve.wait_ge(rt_chain, 5 * g + 2)
                    passed(dve, dve_passed)
                    for s in range(2):
                        nc.vector.max_index(topi[:, 8 * s:8 * s + 8], top[:, 8 * s:8 * s + 8],
                                            logit[:, NE * s:NE * s + NE]).then_inc(rt_chain, 1)
                    dve.wait_ge(rt_chain, 5 * g + 4)
                    nc.vector.tensor_copy(topf[:, :], topi[:, :]).then_inc(rt_chain, 1)
                    ranked = top[:, :].rearrange("p (s j) -> p s j", s=2)
                    nc.vector.tensor_tensor(gsc[:, 0:2].unsqueeze(2), ranked[:, :, 1:2], ranked[:, :, 0:1],
                                            ALU.subtract).then_inc(tops_ready, 1)
                elif what == "GATE":
                    dve.wait_ge(gexp_ready, g + 1)
                    dve.wait_ge(rt_chain, 5 * g + 5)
                    nc.vector.tensor_scalar(gsc[:, 4:6], gsc[:, 2:4], 1.0, None, ALU.add).then_inc(ga_chain, 1)
                    dve.wait_ge(ga_chain, 6 * g + 1)
                    nc.vector.reciprocal(gsc[:, 4:6], gsc[:, 4:6]).then_inc(ga_chain, 1)
                    dve.wait_ge(ga_chain, 6 * g + 2)
                    nc.vector.tensor_tensor(gsc[:, 2:4], gsc[:, 2:4], gsc[:, 4:6], ALU.mult).then_inc(ga_chain, 1)
                    dve.wait_ge(ga_chain, 6 * g + 3)
                    for s in range(2):
                        nc.vector.tensor_scalar(gate2[:, NE * s:NE * s + NE], iota8[:, :], topf[:, 8 * s + 1:8 * s + 2],
                                                gsc[:, 2 + s:3 + s], ALU.is_equal, ALU.mult).then_inc(ga_chain, 1)
                    need(dve, pe["GT"], g)
                    for s in range(2):
                        last = nc.vector.tensor_scalar(gate[:, NE * s:NE * s + NE], iota8[:, :], topf[:, 8 * s:8 * s + 1],
                                                       gsc[:, 4 + s:5 + s], ALU.is_equal, ALU.mult)
                    last.then_inc(ga_chain, 1)
                    dve.wait_ge(ga_chain, 6 * g + 6)
                    nc.vector.tensor_tensor(gate[:, :], gate[:, :], gate2[:, :], ALU.add).then_inc(gate_ready, 1)
                elif what == "GT":
                    dve.wait_ge(pe["GT"], g + 1)
                    need(dve, pe["GB"], 4 * g)
                    nc.vector.tensor_copy(g_t[0][:, :], F[0:NE, 0:N2]).then_inc(gate_copied, 1)
                    dve.wait_ge(gate_copied, g + 1)
                    nc.vector.tensor_tensor(g_t[1][:, :], F[0:NE, 0:N2], g_t[0][:, :].bitcast(F32),
                                            ALU.subtract).then_inc(ev["GT"], 1)
                elif what == "GB":
                    dve.wait_ge(pe["GB"], 4 * g + n + 1)
                    dve.wait_ge(ev["FC"], 4 * g + n + 1)
                    h = at[:, n * 512:(n + 1) * 512]
                    nc.vector.tensor_tensor(h, h, F[:, :], ALU.mult).then_inc(ev["GB"], 1)
                    dve.wait_ge(ev["GB"], 4 * g + n + 1)
                    need(dve, pe["MO"], 4 * g + n)
                    nc.vector.tensor_copy(hg[0][:, :], h).then_inc(h_hi, 1)
                elif what == "LN3":
                    dve.wait_ge(pe["MO"], 4 * g + 4)
                    need(dve, ln_done[0], i + 1 if live(i) else NG)
                    norm_stats(MOB[:, :], x2[:, :], g, 2, ev["MO"])
                    norm_apply(x2, g, 2)

            def mask(i, k):
                got = heads_at(i, k)
                if got is None:
                    return
                kind, g, m = got
                dve.wait_ge(scores[kind], 8 * g + m + 1)
                if kind == "A":
                    dve.wait_ge(bias_r[m], 16 * (g + 1))
                back = heads_before(i, k, 2)
                if back:
                    need(dve, turned[back[0]], 8 * back[1] + back[2] + 1)
                passed(dve, dve_passed)
                for h in range(4):
                    add = bias[m % 4][:, h * T:(h + 1) * T] if kind == "A" else xmask[:, :]
                    nc.vector.tensor_tensor_reduce(prob[k % 2][:, h * T:(h + 1) * T], S[k % 2][:, h * T:(h + 1) * T], add,
                                                   1.0, 3.0e38, ALU.add, ALU.min,
                                                   low[k % 2][:, h:h + 1]).then_inc(masked[kind], 1)

            def invert(i, k):
                got = heads_at(i, k)
                if got is None:
                    return
                kind, g, m = got
                dve.wait_ge(exped[kind], 32 * g + 4 * m + 4)
                nc.vector.reciprocal(inv[k % 2][:, :], total[k % 2][:, :]).then_inc(inved[kind], 1)

            def prob_copy(i, k):
                got = heads_at(i, k)
                if got is None:
                    return
                kind, g, m = got
                dve.wait_ge(turned[kind], 8 * g + m + 1)
                back = heads_before(i, k, 2)
                if back:
                    need(dve, summed[back[0]], 8 * back[1] + back[2] + 1)
                nc.vector.tensor_copy(prob_t[k % 2][:, :], TP[k % 2][:, :]).then_inc(prob_out[kind], 1)

            def one_round(i):
                for k in range(SLOTS):
                    mask(i, k + 1)
                    for it in FILL[k][0]:
                        item(i, *it)
                    prob_copy(i, k)
                    invert(i, k + 1)
                    for it in FILL[k][1]:
                        item(i, *it)

            rounds(dve, one_round)

        @block.gpsimd
        def _(pool):
            nc.gpsimd.memset(c_s[0][:, :], 0.0).then_inc(const_pool, 1)
            nc.gpsimd.memset(c_s[1][:, :], BIG).then_inc(const_pool, 1)
            nc.gpsimd.memset(vx[:, :], 0.0).then_inc(const_pool, 1)
            for j in range(2):
                nc.gpsimd.memset(k_t[j][:, :], 0.0).then_inc(const_pool, 1)
            pool.wait_ge(ld_c[3], 16)
            pool.wait_ge(ld_c[19], 16)
            pool.wait_ge(const_dve, 6)

            def root(g, which):
                pool.wait_ge(stats_ready[which], 2 * g + 2)
                passed(pool, pool_passed)
                r = rstd[which]
                nc.gpsimd.tensor_scalar(r[:, 0:2], mv[:, 1:4:2], EPS, 1.0, ALU.add, ALU.mult).then_inc(eps_added[which], 1)
                pool.wait_ge(eps_added[which], g + 1)
                nc.gpsimd.tensor_tensor(r[:, 2:4], r[:, 0:2], halfpow[:, :], ALU.pow).then_inc(rstd_ready[which], 1)

            def item(i, what, n, off):
                g = i + off
                if not live(g):
                    return
                if what == "XS":
                    pool.wait_ge(x_split, g + 1)
                    nc.gpsimd.tensor_tensor(xt[1][:, :], raw[:, :], xt[0][:, :].bitcast(F32), ALU.subtract).then_inc(x_split_lo, 1)
                elif what == "CS":
                    pool.wait_ge(c_split, g + 1)
                    nc.gpsimd.tensor_tensor(ct[1][:, :], raw[:, :], ct[0][:, :].bitcast(F32), ALU.subtract).then_inc(c_split_lo, 1)
                elif what == "WP":
                    root(g, 0)
                elif what == "WO":
                    root(g, 1)
                elif what == "LN3":
                    root(g, 2)
                elif what == "X1C":
                    pool.wait_ge(ln_done[0], g + 1)
                    need(pool, ev["WO"], g)
                    passed(pool, pool_passed)
                    nc.gpsimd.tensor_scalar(x1_old[:, :], x1[:, :], 1.0, 1.0, ALU.mult, ALU.mult).then_inc(x1_kept, 1)
                elif what == "GB":
                    pool.wait_ge(h_hi, 4 * g + n + 1)
                    nc.gpsimd.tensor_tensor(hg[1][:, :], at[:, n * 512:(n + 1) * 512], hg[0][:, :].bitcast(F32),
                                            ALU.subtract).then_inc(h_lo, 1)

            def normalise(i, k):
                got = heads_at(i, k)
                if got is None:
                    return
                kind, g, m = got
                pool.wait_ge(inved[kind], 8 * g + m + 1)
                p = prob[k % 2][:, :].rearrange("p (h t) -> p h t", h=4)
                nc.gpsimd.tensor_tensor(p, p, inv[k % 2][:, :].unsqueeze(2).to_broadcast([P, 4, T]), ALU.mult).then_inc(normed[kind], 1)

            def one_round(i):
                for k in range(SLOTS):
                    if k == 1 and live(i):
                        pool.wait_ge(ld_xn, 16 * (i + 1))
                        xs = xn[:, :].rearrange("p (s e) -> p s e", s=2)
                        nc.gpsimd.tensor_tensor(xs, xs, bproj_s[:, :].unsqueeze(1).to_broadcast([P, 2, E]), ALU.add).then_inc(xn_ready, 1)
                    for it in FILL[k][0]:
                        item(i, *it)
                    normalise(i, k + 1)
                    for it in FILL[k][1]:
                        item(i, *it)

            rounds(pool, one_round)


def kernel(**inputs):
    import numpy as np
    import concourse.bacc as bacc
    from concourse.bass_utils import run_bass_kernel_spmd

    a = {k: np.asarray(v) for k, v in inputs.items()}
    B, T, E = a["x"].shape
    NE = a["L0_ffn_w_gate"].shape[0]
    nb = a["L0_attn_b_nd"].shape[0]
    tokens_last = lambda v: np.ascontiguousarray(v.reshape(B * T, E).T)
    t = np.arange(P)
    row3 = t // (4 * nb)
    consts = np.zeros((P, 3 * P + 16), np.float32)
    consts[:, 0:P] = np.eye(P)
    consts[:, P:2 * P] = np.where(t[None, :] < P - 1 - t[:, None], BIG, 0.0)
    consts[:, 2 * P:3 * P] = np.where(t[None, :] > t[:, None], BIG, 0.0)
    consts[:, 3 * P + 0] = t % 32 < 16
    consts[:, 3 * P + 1] = t % 32 >= 16
    consts[:, 3 * P + 2] = np.where(row3 == 1, -1.0, 1.0)
    consts[:, 3 * P + 3] = row3 == 1
    consts[:, 3 * P + 4] = np.where(row3 == 2, -1.0, 1.0)
    consts[:, 3 * P + 5] = row3 == 2
    consts[:, 3 * P + 6:3 * P + 8] = -0.5
    consts[:, 3 * P + 8:3 * P + 8 + NE] = np.arange(NE)
    arrays = {
        "x": a["x"], "x_t": tokens_last(a["x"]), "ctx_t": tokens_last(a["ctx_1024"]),
        "wq": a["L0_attn_Wq"], "bq": a["L0_attn_bq"].reshape(-1, P).T, "wk": a["L0_attn_Wk"], "wv": a["L0_attn_Wv"],
        "wproj": a["L0_attn_Wproj"], "bproj": a["L0_attn_bproj"], "wr": a["L0_attn_Wr"], "br": a["L0_attn_br"].reshape(4, -1).T,
        "b_rev": a["L0_attn_b_nd"][:, T - 1::-1],
        "xwq_t": a["L0_xattn_Wq"].T, "xwk_t": a["L0_xattn_Wk"].T, "xwv_t": a["L0_xattn_Wv"].T, "xwo_t": a["L0_xattn_Wo"].T,
        "wg_t": a["L0_ffn_w_gate"].T, "wfc_t": a["L0_ffn_w_fc"].transpose(2, 0, 1), "wpj_t": a["L0_ffn_w_proj"].transpose(2, 0, 1),
        "consts": consts,
    }
    arrays = {k: np.ascontiguousarray(v) for k, v in arrays.items()}
    nc = bacc.Bacc("TRN2", target_bir_lowering=False, num_devices=1)
    aps = {k: nc.dram_tensor(f"in_{k}", v.shape, mybir.dt.from_np(v.dtype), kind="ExternalInput").ap() for k, v in arrays.items()}
    out = nc.dram_tensor("out", (B, T, E), F32, kind="ExternalOutput").ap()
    decoder_kernel(nc, **aps, out=out)
    r = run_bass_kernel_spmd(nc, [{f"in_{k}": v for k, v in arrays.items()}], core_ids=[0])
    return r.results[0]["out"]
```

```python
from contextlib import ExitStack

import concourse.bass as bass
from concourse import mybir

F32 = mybir.dt.float32
F32R = mybir.dt.float32r
U32 = mybir.dt.uint32
ALU = mybir.AluOpType
ACT = mybir.ActivationFunctionType

P = 128
BIG = 1.0e9
EPS = 1e-5

FILL = [
    ([], [("MOT", 0, -3), ("WO", 0, -2)]),
    ([("Q", 2, 0), ("WON", 0, -2)], [("LN3", 0, -3), ("QX", 0, -1), ("WOT", 0, -2)]),
    ([("K", 2, 0), ("LN2", 0, -2)], [("V", 2, 0), ("X2T", 0, -2), ("X2L", 0, -2)]),
    ([("Q", 3, 0)], [("KX", 0, -1), ("RT", 0, -2)]),
    ([("K", 3, 0), ("GX", 0, -2)], [("V", 3, 0), ("XS", 0, 1), ("GA", 0, -2)]),
    ([], [("VX", 0, -1), ("R", 0, 1), ("GATE", 0, -2)]),
    ([("Q", 0, 1), ("RS", 0, 1)], [("K", 0, 1), ("GT", 0, -2)]),
    ([("R", 1, 1), ("X1C", 0, -1)], [("V", 0, 1), ("C", 0, 1), ("RS", 1, 1)]),
    ([("C", 1, 1), ("WP", 0, 0)], [("R", 2, 1), ("C", 2, 1), ("RS", 2, 1)]),
    ([("C", 3, 1)], [("R", 3, 1), ("C", 4, 1), ("RS", 3, 1)]),
    ([("C", 5, 1), ("WP", 1, 0), ("FC", 0, -2)],
     [("FC", 1, -2), ("WPN", 0, 0), ("GB", 0, -2), ("FC", 2, -2), ("HG", 0, -2), ("FC", 3, -2), ("WPT", 0, 0)]),
    ([("GB", 1, -2), ("LN1", 0, 0)], [("HG", 1, -2), ("Q", 1, 1), ("X1T", 0, 0), ("X1L", 0, 0)]),
    ([("GB", 2, -2)], [("MO", 0, -2), ("C", 6, 1), ("HG", 2, -2)]),
    ([("GB", 3, -2), ("K", 1, 1)], [("MO", 1, -2), ("C", 7, 1), ("HG", 3, -2)]),
    ([("V", 1, 1), ("CS", 0, 0)], [("MO", 2, -2)]),
    ([], [("MO", 3, -2), ("MON", 0, -2)]),
]
SLOTS = len(FILL)
BANKED = {"Q": 4, "K": 4, "V": 4, "R": 4, "C": 8, "X1T": 1, "QX": 1, "KX": 1, "VX": 1,
          "WO": 1, "X2T": 1, "RT": 1, "GT": 1, "FC": 4, "GB": 4}
BANK_ORDER = [it for a, b in FILL for it in a + b if it[0] in BANKED]
BANK = {(w, n): j % 2 for j, (w, n, _) in enumerate(BANK_ORDER)}


def decoder_kernel(nc, x, x_t, ctx_t, wq, bq, wk, wv, wproj, bproj, wr, br, b_rev,
                   xwq_t, xwk_t, xwv_t, xwo_t, wg_t, wfc_t, wpj_t, consts, out):
    B, T, E = x.shape
    NG = B // 2
    HD = wq.shape[1]
    H = 16
    DQ = HD // H
    NB = b_rev.shape[0]
    NE, I = wfc_t.shape[1], wfc_t.shape[2]
    XD = E // H
    KC = E // P
    N2 = 2 * T
    LO_ROW = 32
    GR = LO_ROW + NE
    RW = 4 * NB
    R3 = 3 * RW
    ROW = 4 * T + T
    assert T == P and E == 2 * P and DQ == 64 and XD == 16 and I == P and NE == 8 and R3 <= P

    scratch = nc.dram_tensor("bias_scratch", [8, T * ROW], F32, kind="Internal").ap()

    with ExitStack() as es:
        def sb(name, cols, dt=F32, parts=P):
            return es.enter_context(nc.sbuf_tensor(name, [parts, cols], dt))

        def ps(name):
            return es.enter_context(nc.psum_tensor(name, [P, 512], F32))

        def sem(name):
            return es.enter_context(nc.semaphore(name))

        def pair(name, cols):
            return sb(name + "_hi", cols, F32R), sb(name + "_lo", cols, F32R)

        wq_s, wk_s, wv_s = (pair(n, KC * HD) for n in ("wq_s", "wk_s", "wv_s"))
        xwq_s, xwk_s, xwv_s = (pair(n, KC * E) for n in ("xwq_s", "xwk_s", "xwv_s"))
        wr_s = pair("wr_s", KC * 4 * R3)
        wfc_s, wpj_s = pair("wfc_s", KC * NE * I), pair("wpj_s", NE * E)
        wg_s = sb("wg_s", KC * 2 * NE, F32R)
        wp_s = sb("wp_s", (HD // P) * E)
        wo_s = sb("wo_s", KC * E)
        bq_s = sb("bq_s", HD // P)
        br_s = sb("br_s", 4)
        bproj_s = sb("bproj_s", E)
        toep = sb("toep", 4 * T, F32R)
        const = sb("const", consts.shape[1])
        ident, cmask, xmask = const[:, 0:P], const[:, P:2 * P], const[:, 2 * P:3 * P]
        pick, halfpow, iota8 = const[:, 3 * P:3 * P + 6], const[:, 3 * P + 6:3 * P + 8], const[:, 3 * P + 8:3 * P + 16]
        one_r = sb("one_r", NE, F32R, GR)
        raw = sb("raw", KC * N2)
        xt = pair("xt", KC * N2)
        ct = pair("ct", KC * N2)
        qkv = sb("qkv", 2 * 1024)
        q_t, v_s = qkv[:, 0:1024], qkv[:, 1024:2048]
        k_t = [sb(f"k_t{j}", 1024) for j in range(2)]
        at = sb("at", 8 * N2)
        r_st = [sb(f"r_st{j}", N2, F32R) for j in range(2)]
        c_s = [sb(f"c_s{j}", 4 * T) for j in range(2)]
        bias = [sb(f"bias{j}", 4 * T) for j in range(3)]
        prob = [sb(f"prob{j}", 4 * T) for j in range(2)]
        prob_t = [sb(f"prob_t{j}", 4 * T) for j in range(2)]
        low = [sb(f"low{j}", 4) for j in range(2)]
        total = [sb(f"total{j}", 4) for j in range(2)]
        inv = [sb(f"inv{j}", 4) for j in range(2)]
        xn = sb("xn", 2 * E)
        y = sb("y", 2 * E)
        r_f = y[:, 0:N2]
        stat = sb("stat", 2 * 6)
        mv = sb("mv", 2 * 2)
        rstd = [sb(f"rstd{n}", 4) for n in (1, 2, 3)]
        x1 = sb("x1", 2 * E)
        x1_old = sb("x1_old", 2 * E)
        x1_t = pair("x1_t", KC * N2)
        qx = sb("qx", KC * N2)
        kx = [sb(f"kx{j}", KC * N2) for j in range(2)]
        vx = sb("vx", 2 * H * 2 * XD)
        ax = sb("ax", KC * N2)
        x2 = sb("x2", 2 * E)
        x2_t = pair("x2_t", KC * N2)
        logit = sb("logit", 2 * NE)
        top = sb("top", 2 * 8)
        topi = sb("topi", 2 * 8, U32)
        topf = sb("topf", 2 * 8)
        gsc = sb("gsc", 8)
        gate_1, gate_2 = sb("gate_1", 2 * NE), sb("gate_2", 2 * NE)
        gate = sb("gate", 2 * GR)
        g_t = sb("g_t", N2, F32R, GR)
        hg = [sb(f"hg{j}", 2 * N2, F32R) for j in range(3)]
        hg_hi, hg_lo = [hg[0], hg[1], x2_t[0]], [hg[2], x2_t[1]]

        S = [ps("ps_s0"), ps("ps_s1")]
        TP = [ps("ps_t0"), ps("ps_t1")]
        AV = ps("ps_av")
        FB = [ps("ps_f0"), ps("ps_f1")]
        MOB = ps("ps_mo")

        pe = {w: sem(f"pe_{w}") for w in list(BANKED) + ["WP", "MO"]}
        ev = {w: sem(f"ev_{w}") for w in list(BANKED) + ["WP", "MO"]}
        scores = {h: sem(f"scores_{h}") for h in "AB"}
        masked = {h: sem(f"masked_{h}") for h in "AB"}
        exped = {h: sem(f"exped_{h}") for h in "AB"}
        inved = {h: sem(f"inved_{h}") for h in "AB"}
        normed = {h: sem(f"normed_{h}") for h in "AB"}
        turned = {h: sem(f"turned_{h}") for h in "AB"}
        prob_out = {h: sem(f"prob_out_{h}") for h in "AB"}
        summed = {h: sem(f"summed_{h}") for h in "AB"}
        av_out = {h: sem(f"av_out_{h}") for h in "AB"}
        x_split, x_split_lo = sem("x_split"), sem("x_split_lo")
        c_split, c_split_lo = sem("c_split"), sem("c_split_lo")
        r_rounded = sem("r_rounded")
        x1t_hi, x2t_hi = sem("x1t_hi"), sem("x2t_hi")
        xn_ready, x1_kept = sem("xn_ready"), sem("x1_kept")
        stats_ready = [sem(f"stats_ready{n}") for n in (1, 2, 3)]
        rstd_ready = [sem(f"rstd_ready{n}") for n in (1, 2, 3)]
        ln_done = [sem(f"ln_done{n}") for n in (1, 2, 3)]
        tops_ready, gexp_ready, gate_ready = sem("tops_ready"), sem("gexp_ready"), sem("gate_ready")
        gate_copied = sem("gate_copied")
        h_hi, h_lo = sem("h_hi"), sem("h_lo")
        ld_xt, ld_xn, ld_ct, st_out = sem("ld_xt"), sem("ld_xn"), sem("ld_ct"), sem("st_out")
        bias_w = [sem(f"bias_w{k}") for k in range(8)]
        bias_r = [sem(f"bias_r{k}") for k in range(8)]
        ld_w = [sem(f"ld_w{j}") for j in range(2)]
        w_hi, w_lo = sem("w_hi"), sem("w_lo")
        ld_c = [sem(f"ld_c{j}") for j in range(24)]
        const_pool, const_dve = sem("const_pool"), sem("const_dve")
        pad_w = sem("pad_w")
        dve_passed, pool_passed, sp_passed, te_passed = (sem(f"{e}_passed") for e in ("dve", "pool", "sp", "te"))
        ev_rs = sem("ev_rs")
        rt_chain, ga_chain = sem("rt_chain"), sem("ga_chain")
        ln_chain = [sem(f"ln_chain{n}") for n in (1, 2, 3)]
        eps_added = [sem(f"eps_added{n}") for n in (1, 2, 3)]

        def live(g):
            return not isinstance(g, int) or 0 <= g < NG

        def need(eng, s, value):
            if not isinstance(value, int) or value > 0:
                eng.wait_ge(s, value)

        def passed(eng, mark):
            eng.sem_inc(mark, 1)

        def heads_at(i, k):
            if k >= SLOTS:
                i, k = i + 1, k - SLOTS
            if k < 0:
                i, k = i - 1, k + SLOTS
            g = i if k < 8 else i - 1
            return ("A" if k < 8 else "B", g, k % 8) if live(g) else None

        def heads_before(i, k, d):
            k -= d
            while True:
                got = heads_at(i, k)
                if got or not isinstance(i, int):
                    return got
                k -= 8
                if 16 * i + k < 0:
                    return None
                while k < 0:
                    i, k = i - 1, k + SLOTS

        def rounds(eng, one_round):
            for i in (-1, 0, 1, 2):
                one_round(i)
            with eng.Fori(3, NG - 1) as i:
                one_round(i)
            for i in (NG - 1, NG, NG + 1, NG + 2):
                one_round(i)

        wq_d = wq.rearrange("(k p) n -> p k n", p=P)
        wk_d = wk.rearrange("(k p) n -> p k n", p=P)
        wv_d = wv.rearrange("(k p) n -> p k n", p=P)
        split_w = [
            (wq_d, wq_s, KC * HD, -1.0 / 8.0),
            (wk_d, wk_s, KC * HD, 1.0),
            (wv_d, wv_s, KC * HD, 1.0),
            (wr, wr_s, KC * 4 * R3, 1.0),
            (xwq_t.rearrange("(k p) n -> p k n", p=P), xwq_s, KC * E, -1.0 / 4.0),
            (xwk_t.rearrange("(k p) n -> p k n", p=P), xwk_s, KC * E, 1.0),
            (xwv_t.rearrange("(k p) n -> p k n", p=P), xwv_s, KC * E, 1.0),
            (wfc_t.rearrange("(k p) e i -> p k (e i)", p=P), wfc_s, KC * NE * I, 1.0),
            (wpj_t.rearrange("p e n -> p (e n)"), wpj_s, NE * E, 1.0),
            (wg_t.rearrange("(k p) n -> p k n", p=P), [wg_s[:, :].rearrange("p (k d n) -> p k d n", k=KC, d=2)[:, :, d, :] for d in range(2)], KC * NE, 1.0),
        ]
        stages = [at[:, 0:2048], qkv[:, 0:2048]]
        NW = len(split_w)

        def stage(n, dst):
            flat = stages[n % 2][:, 0:split_w[n][2]]
            return flat.rearrange("p (k n) -> p k n", k=KC) if len(dst.shape) == 3 else flat

        x_g = x.rearrange("(g s) t e -> g t s e", s=2)
        out_g = out.rearrange("(g s) t e -> g t s e", s=2)
        xt_g = x_t.rearrange("(k p) (g n) -> g p k n", p=P, n=N2)
        ct_g = ctx_t.rearrange("(k p) (g n) -> g p k n", p=P, n=N2)

        block = es.enter_context(nc.Block())

        @block.sync
        def _(sp):
            for n, (src, _, cols, _) in enumerate(split_w):
                if n >= 2:
                    sp.wait_ge(w_lo, n - 1)
                if src is wr:
                    for d in range(3):
                        for k in range(KC):
                            dst = stages[n % 2][:, k * 4 * R3:(k + 1) * 4 * R3].rearrange("p (b d n) -> p b d n", b=4, d=3)
                            sp.dma_start(dst[:, :, d, :], wr[k * P:(k + 1) * P, :].rearrange("p (b n) -> p b n", b=4)
                                         ).then_inc(ld_w[n % 2], 16)
                else:
                    dst = stages[n % 2][:, 0:cols]
                    if len(src.shape) == 3:
                        dst = dst.rearrange("p (k n) -> p k n", k=KC)
                    sp.dma_start(dst, src).then_inc(ld_w[n % 2], 16)
                if n == 0:
                    sp.dma_start(const[:, :], consts[:, :]).then_inc(ld_c[19], 16)
                    sp.dma_start(wp_s[:, :].rearrange("p (c n) -> p c n", n=E),
                                 wproj.rearrange("(c p) n -> p c n", p=P)).then_inc(ld_c[0], 16)
                    sp.dma_start(wo_s[:, :].rearrange("p (c n) -> p c n", n=E),
                                 xwo_t.rearrange("(c p) n -> p c n", p=P)).then_inc(ld_c[1], 16)
                    sp.dma_start(bq_s[:, :], bq[:, :]).then_inc(ld_c[2], 16)
                    sp.dma_start(bproj_s[:, :], bproj.rearrange("(a n) -> a n", a=1).to_broadcast([P, E])).then_inc(ld_c[3], 16)
                    for d in range(3):
                        sp.dma_start(br_s[d * RW:(d + 1) * RW, :], br[:, :]).then_inc(ld_c[4 + d], 16)
                    sp.wait_ge(const_pool, 3)
                    for d in range(3):
                        for h in range(4):
                            sp.dma_start(c_s[0][d * RW + h * NB:d * RW + (h + 1) * NB, h * T:(h + 1) * T],
                                         b_rev[:, :]).then_inc(ld_c[7 + 4 * d + h], 16)
                    for k in range(8):
                        sp.dma_start(scratch[k, :].rearrange("(t w) -> t w", w=ROW)[:, 4 * T:ROW],
                                     c_s[1][:, 0:T]).then_inc(pad_w, 16)

            def one_round(i):
                for k in range(SLOTS):
                    if k == 4 and live(i):
                        need(sp, st_out, 16 * (i - 2))
                        sp.dma_start(xn[:, :].rearrange("p (s e) -> p s e", s=2), x_g[i]).then_inc(ld_xn, 16)
                    if k == 0 and live(i + 1):
                        need(sp, c_split, i)
                        need(sp, c_split_lo, i)
                        sp.dma_start(raw[:, :].rearrange("p (k n) -> p k n", k=KC), xt_g[i + 1]).then_inc(ld_xt, 16)
                    if k == 6 and live(i):
                        need(sp, x_split, i + 2 if live(i + 1) else NG)
                        need(sp, x_split_lo, i + 2 if live(i + 1) else NG)
                        sp.dma_start(raw[:, :].rearrange("p (k n) -> p k n", k=KC), ct_g[i]).then_inc(ld_ct, 16)
                    for what, n, off in FILL[k][0] + FILL[k][1]:
                        if what == "C" and live(i + off):
                            need(sp, ev["C"], 8 * (i + off) + n + 1)
                            passed(sp, sp_passed)
                            need(sp, bias_r[n], 16 * (i + off))
                            if isinstance(i, int) and i + off == 0 and n == 0:
                                sp.wait_ge(pad_w, 128)
                            sp.dma_start(scratch[n, :].rearrange("(t w) -> t w", w=ROW)[:, 0:4 * T],
                                         c_s[n % 2][:, :]).then_inc(bias_w[n], 16)
                    g, m = (i, k + 3) if k < 5 else (i + 1, k - 13)
                    if (k < 5 or k >= 13) and live(g):
                        sp.wait_ge(bias_w[m], 16 * (g + 1))
                        passed(sp, sp_passed)
                        need(sp, masked["A"], 32 * g + 4 * (m - 3) + 4 if m >= 3 else 32 * g)
                        sp.dma_start(bias[m % 3][:, :],
                                     scratch[m, T - 1:T - 1 + T * (ROW - 1)].rearrange("(t w) -> t w", w=ROW - 1)[:, 0:4 * T]
                                     ).then_inc(bias_r[m], 16)
                    if k == 2 and live(i - 3):
                        sp.wait_ge(ln_done[2], i - 2)
                        sp.dma_start(out_g[i - 3], xn[:, :].rearrange("p (s e) -> p s e", s=2)).then_inc(st_out, 16)

            rounds(sp, one_round)
            sp.wait_ge(st_out, 16 * NG)

        @block.tensor
        def _(te):
            te.wait_ge(w_lo, NW)
            te.wait_ge(const_dve, 7)
            te.wait_ge(const_pool, 6)
            te.wait_ge(ld_c[19], 16)
            te.wait_ge(ld_c[0], 16)
            te.wait_ge(ld_c[1], 16)
            users = [None, None]

            def free_bank(i, what, n):
                b = BANK[(what, n)]
                if users[b] is not None:
                    w, m, g = users[b]
                    need(te, ev[w], BANKED[w] * g + m + 1)
                return FB[b]

            def three(out_ap, stationary, moving, first, last):
                nc.tensor.matmul(out_ap, stationary(0), moving(0), start=first, stop=False)
                nc.tensor.matmul(out_ap, stationary(0), moving(1), start=False, stop=False)
                return nc.tensor.matmul(out_ap, stationary(1), moving(0), start=False, stop=last)

            def k3(t, k, n):
                return t[:, k * n:(k + 1) * n]

            def item(i, what, n, off):
                g = i + off
                if not live(g):
                    return
                if what == "MO":
                    te.wait_ge(h_hi, 4 * g + n + 1)
                    te.wait_ge(h_lo, 4 * g + n + 1)
                    if n == 0:
                        te.wait_ge(ev["WP"], i + 1 if live(i) else NG)
                    h = (hg_hi[n % 3], hg_lo[n % 2])
                    for e in range(2):
                        for s in range(2):
                            for a, b in ((0, 0), (0, 1), (1, 0)):
                                last = nc.tensor.matmul(
                                    MOB[:, s * E:(s + 1) * E], h[a][:, e * N2 + s * T:e * N2 + (s + 1) * T],
                                    k3(wpj_s[b], 2 * n + e, E), start=(n == 0 and e == 0 and s == 0 and a == 0 and b == 0),
                                    stop=(n == 3 and e == 1 and a == 1), skip_group_check=True)
                    last.then_inc(pe["MO"], 1)
                    return
                if what == "WP":
                    te.wait_ge(av_out["A"], 8 * g + 7 + n)
                    if n == 0:
                        need(te, ev["MO"], g - 2)
                    for c in range(8):
                        last = nc.tensor.matmul(MOB[:, n * E:(n + 1) * E], at[:, c * N2 + n * T:c * N2 + (n + 1) * T],
                                                wp_s[:, c * E:(c + 1) * E], start=c == 0, stop=c == 7)
                    if n == 1:
                        last.then_inc(pe["WP"], 1)
                    return
                if what not in BANKED:
                    return
                F = free_bank(i, what, n)
                if what in "QK":
                    if n == 0:
                        te.wait_ge(x_split_lo, g + 1)
                    w = wq_s if what == "Q" else wk_s
                    for j in range(2):
                        c = 2 * n + j
                        for k in range(KC):
                            last = three(F[:, j * N2:(j + 1) * N2],
                                         lambda a: w[a][:, k * HD + c * P:k * HD + (c + 1) * P],
                                         lambda a: k3(xt[a], k, N2), k == 0, k == KC - 1)
                elif what == "V":
                    for s in range(2):
                        for k in range(KC):
                            last = three(F[:, s * 256:(s + 1) * 256],
                                         lambda a: xt[a][:, k * N2 + s * T:k * N2 + (s + 1) * T],
                                         lambda a: wv_s[a][:, k * HD + n * 256:k * HD + (n + 1) * 256], k == 0, k == KC - 1)
                elif what == "R":
                    te.wait_ge(x_split_lo, g + 1)
                    for k in range(KC):
                        last = three(F[0:R3, 0:N2],
                                     lambda a: wr_s[a][:, (k * 4 + n) * R3:(k * 4 + n + 1) * R3],
                                     lambda a: k3(xt[a], k, N2), k == 0, k == KC - 1)
                elif what == "C":
                    hb, s = n // 2, n % 2
                    te.wait_ge(ev_rs, 4 * g + hb + 1)
                    last = nc.tensor.matmul(F[:, :], r_st[hb % 2][0:R3, s * T:(s + 1) * T], toep[0:R3, :],
                                            start=True, stop=True)
                elif what in ("X1T", "X2T"):
                    src, done = (x1, ln_done[0]) if what == "X1T" else (x2, ln_done[1])
                    te.wait_ge(done, g + 1)
                    for k in range(KC):
                        for s in range(2):
                            last = nc.tensor.transpose(F[:, k * N2 + s * T:k * N2 + (s + 1) * T],
                                                       src[:, s * E + k * P:s * E + (k + 1) * P], ident[:, :])
                elif what in ("QX", "KX"):
                    if what == "QX":
                        te.wait_ge(ev["X1T"], g + 1)
                    else:
                        te.wait_ge(c_split_lo, g + 1)
                    w, mov = (xwq_s, x1_t) if what == "QX" else (xwk_s, ct)
                    for c in range(KC):
                        for k in range(KC):
                            last = three(F[:, c * N2:(c + 1) * N2],
                                         lambda a: w[a][:, k * E + c * P:k * E + (c + 1) * P],
                                         lambda a: k3(mov[a], k, N2), k == 0, k == KC - 1)
                elif what == "VX":
                    te.wait_ge(c_split_lo, g + 1)
                    for s in range(2):
                        for k in range(KC):
                            last = three(F[:, s * E:(s + 1) * E],
                                         lambda a: ct[a][:, k * N2 + s * T:k * N2 + (s + 1) * T],
                                         lambda a: k3(xwv_s[a], k, E), k == 0, k == KC - 1)
                elif what == "WO":
                    te.wait_ge(av_out["B"], 8 * g + 8)
                    for s in range(2):
                        for c in range(KC):
                            last = nc.tensor.matmul(F[:, s * E:(s + 1) * E], ax[:, c * N2 + s * T:c * N2 + (s + 1) * T],
                                                    k3(wo_s, c, E), start=c == 0, stop=c == KC - 1)
                elif what == "RT":
                    te.wait_ge(ev["X2T"], g + 1)
                    for s in range(2):
                        for k in range(KC):
                            nc.tensor.matmul(F[:, 2 * s * NE:2 * (s + 1) * NE], x2_t[0][:, k * N2 + s * T:k * N2 + (s + 1) * T],
                                             wg_s[:, 2 * k * NE:2 * (k + 1) * NE], start=k == 0, stop=False,
                                             skip_group_check=True)
                            last = nc.tensor.matmul(F[:, 2 * s * NE:(2 * s + 1) * NE],
                                                    x2_t[1][:, k * N2 + s * T:k * N2 + (s + 1) * T],
                                                    wg_s[:, 2 * k * NE:(2 * k + 1) * NE], start=False, stop=k == KC - 1,
                                                    skip_group_check=True)
                elif what == "GT":
                    te.wait_ge(gate_ready, 2 * g + 2)
                    passed(te, te_passed)
                    for s in range(2):
                        last = nc.tensor.transpose(F[0:GR, s * T:(s + 1) * T], gate[:, s * GR:(s + 1) * GR], ident[:, :])
                elif what == "GB":
                    te.wait_ge(ev["GT"], g + 1)
                    for e in range(2):
                        last = nc.tensor.matmul(F[:, e * N2:(e + 1) * N2],
                                                one_r[:, 2 * n + e:2 * n + e + 1].to_broadcast([GR, P]), g_t[:, :],
                                                start=True, stop=True)
                elif what == "FC":
                    for e in range(2):
                        for k in range(KC):
                            last = three(F[:, e * N2:(e + 1) * N2],
                                         lambda a: wfc_s[a][:, k * NE * I + (2 * n + e) * I:k * NE * I + (2 * n + e + 1) * I],
                                         lambda a: k3(x2_t[a], k, N2), k == 0, k == KC - 1)
                last.then_inc(pe[what], 1)
                users[BANK[(what, n)]] = (what, n, g)

            def score(i, k):
                got = heads_at(i, k)
                if got is None:
                    return
                kind, g, m = got
                hb, s = m // 2, m % 2
                back = heads_before(i, k, 2)
                if back:
                    need(te, masked[back[0]], 32 * back[1] + 4 * back[2] + 4)
                if kind == "A":
                    te.wait_ge(ev["Q"], 4 * g + hb + 1)
                    te.wait_ge(ev["K"], 4 * g + hb + 1)
                else:
                    te.wait_ge(ev["QX"], g + 1)
                    te.wait_ge(ev["KX"], g + 1)
                for h in range(4):
                    if kind == "A":
                        col = (hb % 2) * 512 + (h // 2) * N2 + s * T
                        lhs, rhs = q_t[:, col:col + T], k_t[h % 2][:, col:col + T]
                    else:
                        r = 32 * hb
                        col = (h // 2) * N2 + s * T
                        lhs, rhs = qx[r:r + 32, col:col + T], kx[h % 2][r:r + 32, col:col + T]
                    last = nc.tensor.matmul(S[k % 2][:, h * T:(h + 1) * T], lhs, rhs, start=True, stop=True)
                last.then_inc(scores[kind], 1)

            def turn(i, k):
                got = heads_at(i, k)
                if got is None:
                    return
                kind, g, m = got
                te.wait_ge(normed[kind], 8 * g + m + 1)
                back = heads_before(i, k, 2)
                if back:
                    need(te, prob_out[back[0]], 8 * back[1] + back[2] + 1)
                for h in range(4):
                    last = nc.tensor.transpose(TP[k % 2][:, h * T:(h + 1) * T], prob[k % 2][:, h * T:(h + 1) * T], ident[:, :])
                last.then_inc(turned[kind], 1)

            def weigh(i, k):
                got = heads_at(i, k)
                if got is None:
                    return
                kind, g, m = got
                hb, s = m // 2, m % 2
                te.wait_ge(prob_out[kind], 8 * g + m + 1)
                back = heads_before(i, k, 1)
                if back:
                    need(te, av_out[back[0]], 8 * back[1] + back[2] + 1)
                if kind == "A":
                    te.wait_ge(ev["V"], 4 * g + hb + 1)
                else:
                    te.wait_ge(ev["VX"], g + 1)
                for h in range(4):
                    rhs = prob_t[k % 2][:, h * T:(h + 1) * T]
                    if kind == "A":
                        col = (hb % 2) * 512 + s * 256 + h * DQ
                        last = nc.tensor.matmul(AV[64 * (h % 2):64 * (h % 2) + 64, (h // 2) * T:(h // 2 + 1) * T],
                                                v_s[:, col:col + DQ], rhs, start=True, stop=True)
                    else:
                        c = h // 2
                        col = s * H * 32 + (8 * c + 2 * hb + h % 2) * 32
                        last = nc.tensor.matmul(AV[32 * hb:32 * hb + 32, c * T:(c + 1) * T], vx[:, col:col + 32], rhs,
                                                start=h % 2 == 0, stop=h % 2 == 1)
                last.then_inc(summed[kind], 1)

            def one_round(i):
                if not isinstance(i, int):
                    for what, n, off in BANK_ORDER[-2:]:
                        users[BANK[(what, n)]] = (what, n, i - 1 + off)
                for k in range(SLOTS):
                    score(i, k + 1)
                    for it in FILL[k][0]:
                        item(i, *it)
                    turn(i, k)
                    for it in FILL[k][1]:
                        item(i, *it)
                    weigh(i, k)
                if not isinstance(i, int):
                    for what, n, off in BANK_ORDER[-2:]:
                        users[BANK[(what, n)]] = (what, n, NG - 2 + off)

            rounds(te, one_round)

        @block.scalar
        def _(act):
            for n, (src, dst, cols, f) in enumerate(split_w):
                act.wait_ge(ld_w[n % 2], 16 * sum(3 * KC if split_w[j][0] is wr else 1 for j in range(n % 2, n + 1, 2)))
                nc.scalar.activation(dst[0][:], stage(n, dst[0]), ACT.Copy, scale=f).then_inc(w_hi, 1)
            act.wait_ge(const_dve, 7)
            for j in range(3):
                act.wait_ge(ld_c[4 + j], 16)
            act.wait_ge(const_pool, 6)
            act.wait_ge(w_lo, NW)

            def item(i, what, n, off):
                g = i + off
                if not live(g):
                    return
                F = FB[BANK[(what, n)]] if what in BANKED else None
                if what == "Q":
                    act.wait_ge(pe["Q"], 4 * g + n + 1)
                    need(act, scores["A"], 8 * g + 2 * (n - 2) + 2)
                    for j in range(2):
                        last = nc.scalar.activation(q_t[:, (n % 2) * 512 + j * N2:(n % 2) * 512 + (j + 1) * N2],
                                                    F[:, j * N2:(j + 1) * N2], ACT.Identity,
                                                    bias=bq_s[:, 2 * n + j:2 * n + j + 1])
                    last.then_inc(ev["Q"], 1)
                elif what == "K":
                    act.wait_ge(pe["K"], 4 * g + n + 1)
                    need(act, scores["A"], 8 * g + 2 * (n - 2) + 2)
                    for j in range(2):
                        last = nc.scalar.activation(k_t[j][64 * j:64 * j + 64, (n % 2) * 512:(n % 2 + 1) * 512],
                                                    F[64 * j:64 * j + 64, :], ACT.Copy)
                    last.then_inc(ev["K"], 1)
                elif what == "V":
                    act.wait_ge(pe["V"], 4 * g + n + 1)
                    need(act, summed["A"], 8 * g + 2 * (n - 2) + 2)
                    nc.scalar.activation(v_s[:, (n % 2) * 512:(n % 2 + 1) * 512], F[:, :], ACT.Copy).then_inc(ev["V"], 1)
                elif what == "R":
                    act.wait_ge(pe["R"], 4 * g + n + 1)
                    need(act, ev_rs, 4 * g + n)
                    nc.scalar.activation(r_f[0:R3, :], F[0:R3, 0:N2], ACT.Identity,
                                         bias=br_s[0:R3, n:n + 1]).then_inc(ev["R"], 1)
                elif what in ("X1T", "X2T"):
                    t, s, last = (x1_t, x1t_hi, pe["QX"]) if what == "X1T" else (x2_t, x2t_hi, pe["FC"])
                    act.wait_ge(pe[what], g + 1)
                    need(act, last, g if what == "X1T" else 4 * g)
                    nc.scalar.activation(t[0][:, :], F[:, :], ACT.Copy).then_inc(s, 1)
                elif what == "QX":
                    act.wait_ge(pe["QX"], g + 1)
                    need(act, scores["B"], 8 * g)
                    nc.scalar.activation(qx[:, :], F[:, :], ACT.Copy).then_inc(ev["QX"], 1)
                elif what == "GX":
                    act.wait_ge(tops_ready, g + 1)
                    nc.scalar.activation(gsc[:, 2:4], gsc[:, 0:2], ACT.Exp).then_inc(gexp_ready, 1)
                elif what == "FC":
                    act.wait_ge(pe["FC"], 4 * g + n + 1)
                    need(act, pe["WP"], (i + 1) if live(i) else NG)
                    nc.scalar.activation(at[:, n * 512:(n + 1) * 512], F[:, :], ACT.Gelu).then_inc(ev["FC"], 1)

            def exps(i, k):
                got = heads_at(i, k)
                if got is None:
                    return
                kind, g, m = got
                p = prob[k % 2]
                for h in range(4):
                    act.wait_ge(masked[kind], 32 * g + 4 * m + h + 1)
                    nc.scalar.activation(p[:, h * T:(h + 1) * T], p[:, h * T:(h + 1) * T], ACT.Exp,
                                         bias=low[k % 2][:, h:h + 1], scale=-1.0,
                                         accum_out=total[k % 2][:, h:h + 1]).then_inc(exped[kind], 1)

            def av(i, k):
                got = heads_at(i, k)
                if got is None:
                    return
                kind, g, m = got
                hb, s = m // 2, m % 2
                act.wait_ge(summed[kind], 8 * g + m + 1)
                if kind == "A":
                    if m == 0:
                        need(act, pe["WP"], g)
                        need(act, h_lo, 4 * (g - 2))
                    dst = at[:, :].rearrange("p (c s t) -> p c s t", c=8, s=2)[:, 2 * hb:2 * hb + 2, s, :]
                    nc.scalar.activation(dst, AV[:, 0:2 * T].rearrange("p (c t) -> p c t", c=2), ACT.Copy).then_inc(av_out["A"], 1)
                else:
                    if m == 0:
                        need(act, pe["WO"], g)
                    r = 32 * hb
                    dst = ax[r:r + 32, :].rearrange("p (c s t) -> p c s t", c=2, s=2)[:, :, s, :]
                    nc.scalar.activation(dst, AV[r:r + 32, 0:2 * T].rearrange("p (c t) -> p c t", c=2), ACT.Copy).then_inc(av_out["B"], 1)

            def one_round(i):
                for k in range(SLOTS):
                    exps(i, k + 1)
                    for it in FILL[k][0] + FILL[k][1]:
                        item(i, *it)
                    av(i, k)

            rounds(act, one_round)

        @block.vector
        def _(dve):
            for n, (src, dst, cols, f) in enumerate(split_w):
                dve.wait_ge(w_hi, n + 1)
                nc.vector.scalar_tensor_tensor(out=dst[1][:], in0=stage(n, dst[0]), scalar=f,
                                               in1=dst[0][:].bitcast(F32), op0=ALU.mult,
                                               op1=ALU.subtract).then_inc(w_lo, 1)
            dve.wait_ge(ld_c[2], 16)
            nc.vector.tensor_scalar(bq_s[:, :], bq_s[:, :], -1.0 / 8.0, None, ALU.mult).then_inc(const_dve, 1)
            for j in range(12):
                dve.wait_ge(ld_c[7 + j], 16)
            dve.wait_ge(ld_c[19], 16)
            nc.vector.tensor_scalar(c_s[0][:, :], c_s[0][:, :], -1.0, None, ALU.mult).then_inc(const_dve, 1)
            dve.wait_ge(const_dve, 2)
            nc.vector.tensor_copy(toep[:, :], c_s[0][:, :]).then_inc(const_dve, 1)
            dve.wait_ge(const_dve, 3)
            nc.vector.tensor_scalar(y[:, :], toep[:, :].bitcast(F32), pick[:, 4:5], None, ALU.mult).then_inc(const_dve, 1)
            dve.wait_ge(const_dve, 4)
            nc.vector.scalar_tensor_tensor(out=toep[:, :], in0=c_s[0][:, :], scalar=pick[:, 5:6], in1=y[:, :],
                                           op0=ALU.mult, op1=ALU.add).then_inc(const_dve, 1)
            nc.vector.tensor_copy(one_r[0:LO_ROW, :], ident[0:LO_ROW, 0:NE]).then_inc(const_dve, 1)
            nc.vector.tensor_copy(one_r[LO_ROW:GR, :], ident[LO_ROW:GR, LO_ROW:GR]).then_inc(const_dve, 1)
            dve.wait_ge(const_dve, 7)
            dve.wait_ge(pad_w, 128)
            dve.wait_ge(const_pool, 6)

            def norm_sum(dst, F, res, n_sem):
                nc.vector.tensor_tensor(dst[:, :], F, res, ALU.add).then_inc(n_sem, 1)

            def norm_stats(src, g, which, n_sem):
                ch = ln_chain[which]
                dve.wait_ge(n_sem, g + 1)
                for s in range(2):
                    nc.vector.bn_stats(stat[:, 6 * s:6 * s + 6], src[:, s * E:(s + 1) * E]).then_inc(ch, 1)
                dve.wait_ge(ch, 2 * g + 2)
                passed(dve, dve_passed)
                for s in range(2):
                    nc.vector.bn_aggr(mv[:, 2 * s:2 * s + 2], stat[:, 6 * s:6 * s + 6]).then_inc(stats_ready[which], 1)

            def norm_apply(dst, src, g, which):
                dve.wait_ge(rstd_ready[which], g + 1)
                for s in range(2):
                    last = nc.vector.tensor_scalar(dst[:, s * E:(s + 1) * E], src[:, s * E:(s + 1) * E],
                                                   mv[:, 2 * s:2 * s + 1], rstd[which][:, 2 + s:3 + s], ALU.subtract, ALU.mult)
                last.then_inc(ln_done[which], 1)

            def item(i, what, n, off):
                g = i + off
                if not live(g):
                    return
                F = FB[BANK[(what, n)]] if what in BANKED else None
                if what == "XS":
                    dve.wait_ge(ld_xt, 16 * (g + 1))
                    need(dve, pe["V"], 4 * g)
                    nc.vector.tensor_copy(xt[0][:, :], raw[:, :]).then_inc(x_split, 1)
                elif what == "CS":
                    dve.wait_ge(ld_ct, 16 * (g + 1))
                    need(dve, pe["VX"], g)
                    nc.vector.tensor_copy(ct[0][:, :], raw[:, :]).then_inc(c_split, 1)
                elif what == "RS":
                    dve.wait_ge(ev["R"], 4 * g + n + 1)
                    need(dve, pe["C"], 8 * g + 2 * (n - 2) + 2)
                    r = r_st[n % 2][0:R3, :]
                    nc.vector.tensor_scalar(r, r_f[0:R3, :], pick[0:R3, 2:3], None, ALU.mult).then_inc(r_rounded, 1)
                    dve.wait_ge(r_rounded, 4 * g + n + 1)
                    nc.vector.scalar_tensor_tensor(out=r, in0=r_f[0:R3, :], scalar=pick[0:R3, 3:4], in1=r.bitcast(F32),
                                                   op0=ALU.mult, op1=ALU.add).then_inc(ev_rs, 1)
                elif what == "C":
                    dve.wait_ge(pe["C"], 8 * g + n + 1)
                    if n >= 2:
                        dve.wait_ge(bias_w[n - 2], 16 * (g + 1))
                    else:
                        need(dve, bias_w[n + 6], 16 * g)
                    nc.vector.tensor_tensor(c_s[n % 2][:, :].rearrange("p (h t) -> p h t", h=4),
                                            F[:, :].rearrange("p (h t) -> p h t", h=4),
                                            cmask[:, :].unsqueeze(1).to_broadcast([P, 4, T]), ALU.add).then_inc(ev["C"], 1)
                elif what == "WPN":
                    dve.wait_ge(pe["WP"], g + 1)
                    dve.wait_ge(xn_ready, g + 1)
                    need(dve, ln_done[1], g - 1)
                    need(dve, ev_rs, 4 * (i + 2 if live(i + 1) else NG))
                    norm_sum(y, MOB[:, :], xn[:, :], ev["WP"])
                elif what == "WPT":
                    norm_stats(y, g, 0, ev["WP"])
                elif what == "LN1":
                    need(dve, x1_kept, g)
                    need(dve, pe["X1T"], g)
                    norm_apply(x1, y, g, 0)
                elif what in ("X1L", "X2L"):
                    w, t, s = ("X1T", x1_t, x1t_hi) if what == "X1L" else ("X2T", x2_t, x2t_hi)
                    dve.wait_ge(s, g + 1)
                    nc.vector.tensor_tensor(t[1][:, :], FB[BANK[(w, 0)]][:, :], t[0][:, :].bitcast(F32),
                                            ALU.subtract).then_inc(ev[w], 1)
                elif what == "KX":
                    dve.wait_ge(pe["KX"], g + 1)
                    need(dve, scores["B"], 8 * g)
                    for j in range(2):
                        last = nc.vector.tensor_scalar(kx[j][:, :], F[:, :], pick[:, j:j + 1], None, ALU.mult)
                    last.then_inc(ev["KX"], 1)
                elif what == "VX":
                    dve.wait_ge(pe["VX"], g + 1)
                    need(dve, summed["B"], 8 * g)
                    for s in range(2):
                        dst = vx[:, s * 512:(s + 1) * 512].rearrange("p (h a d) -> p h a d", a=4, d=XD)[:, :, 0:4:3, :]
                        last = nc.vector.tensor_copy(dst, F[:, s * E:(s + 1) * E].rearrange("p (h a d) -> p h a d", a=2, d=XD))
                    last.then_inc(ev["VX"], 1)
                elif what == "WON":
                    dve.wait_ge(pe["WO"], g + 1)
                    dve.wait_ge(x1_kept, g + 1)
                    need(dve, ln_done[0], i if live(i - 1) else NG)
                    norm_sum(y, FB[BANK[("WO", 0)]][:, :], x1_old[:, :], ev["WO"])
                elif what == "WOT":
                    need(dve, ln_done[2], g)
                    norm_stats(y, g, 1, ev["WO"])
                elif what == "LN2":
                    need(dve, ev["MO"], g)
                    norm_apply(x2, y, g, 1)
                elif what == "RT":
                    dve.wait_ge(pe["RT"], g + 1)
                    parts = F[:, 0:4 * NE].rearrange("p (s d n) -> p s d n", s=2, d=2)
                    nc.vector.tensor_reduce(logit[:, :].rearrange("p (s n) -> p s n", s=2), parts.rearrange("p s d n -> p s n d"),
                                            mybir.AxisListType.X, ALU.add).then_inc(ev["RT"], 1)
                    dve.wait_ge(ev["RT"], g + 1)
                    passed(dve, dve_passed)
                    for s in range(2):
                        nc.vector.max(top[:, 8 * s:8 * s + 8], logit[:, NE * s:NE * s + NE]).then_inc(rt_chain, 1)
                    dve.wait_ge(rt_chain, 5 * g + 2)
                    passed(dve, dve_passed)
                    for s in range(2):
                        nc.vector.max_index(topi[:, 8 * s:8 * s + 8], top[:, 8 * s:8 * s + 8],
                                            logit[:, NE * s:NE * s + NE]).then_inc(rt_chain, 1)
                    dve.wait_ge(rt_chain, 5 * g + 4)
                    nc.vector.tensor_copy(topf[:, :], topi[:, :]).then_inc(rt_chain, 1)
                    ranked = top[:, :].rearrange("p (s j) -> p s j", s=2)
                    nc.vector.tensor_tensor(gsc[:, 0:2].unsqueeze(2), ranked[:, :, 1:2], ranked[:, :, 0:1],
                                            ALU.subtract).then_inc(tops_ready, 1)
                elif what == "GA":
                    dve.wait_ge(gexp_ready, g + 1)
                    dve.wait_ge(rt_chain, 5 * g + 5)
                    nc.vector.tensor_scalar(gsc[:, 4:6], gsc[:, 2:4], 1.0, None, ALU.add).then_inc(ga_chain, 1)
                    dve.wait_ge(ga_chain, 7 * g + 1)
                    nc.vector.reciprocal(gsc[:, 4:6], gsc[:, 4:6]).then_inc(ga_chain, 1)
                    dve.wait_ge(ga_chain, 7 * g + 2)
                    nc.vector.tensor_tensor(gsc[:, 2:4], gsc[:, 2:4], gsc[:, 4:6], ALU.mult).then_inc(ga_chain, 1)
                elif what == "GATE":
                    dve.wait_ge(ga_chain, 7 * g + 3)
                    for t, rank, at_rank in ((gate_1, 0, 4), (gate_2, 1, 2)):
                        for s in range(2):
                            nc.vector.tensor_scalar(t[:, NE * s:NE * s + NE], iota8[:, :], topf[:, 8 * s + rank:8 * s + rank + 1],
                                                    gsc[:, at_rank + s:at_rank + s + 1], ALU.is_equal,
                                                    ALU.mult).then_inc(ga_chain, 1)
                    need(dve, pe["GT"], g)
                    dve.wait_ge(ga_chain, 7 * g + 7)
                    for d in (0, LO_ROW):
                        nc.vector.tensor_tensor(gate[:, :].rearrange("p (s n) -> p s n", s=2)[:, :, d:d + NE],
                                                gate_1[:, :].rearrange("p (s n) -> p s n", s=2),
                                                gate_2[:, :].rearrange("p (s n) -> p s n", s=2), ALU.add).then_inc(gate_ready, 1)
                elif what == "GT":
                    dve.wait_ge(pe["GT"], g + 1)
                    need(dve, pe["GB"], 4 * g)
                    nc.vector.tensor_copy(g_t[:, :], F[0:GR, 0:N2]).then_inc(gate_copied, 1)
                    dve.wait_ge(gate_copied, g + 1)
                    nc.vector.tensor_tensor(g_t[LO_ROW:GR, :], F[LO_ROW:GR, 0:N2], g_t[LO_ROW:GR, :].bitcast(F32),
                                            ALU.subtract).then_inc(ev["GT"], 1)
                elif what == "GB":
                    dve.wait_ge(pe["GB"], 4 * g + n + 1)
                    dve.wait_ge(ev["FC"], 4 * g + n + 1)
                    h = at[:, n * 512:(n + 1) * 512]
                    nc.vector.tensor_tensor(h, h, F[:, :], ALU.mult).then_inc(ev["GB"], 1)
                elif what == "HG":
                    dve.wait_ge(ev["GB"], 4 * g + n + 1)
                    if n == 2:
                        dve.wait_ge(pe["FC"], 4 * g + 4)
                    need(dve, pe["MO"], 4 * g + n - 2)
                    h = at[:, n * 512:(n + 1) * 512]
                    nc.vector.tensor_copy(hg_hi[n % 3][:, :], h).then_inc(h_hi, 1)
                elif what == "MON":
                    dve.wait_ge(pe["MO"], 4 * g + 4)
                    dve.wait_ge(ev["WP"], i + 1 if live(i) else NG)
                    if not live(i):
                        dve.wait_ge(st_out, 16 * g)
                    norm_sum(xn, MOB[:, :], x2[:, :], ev["MO"])
                elif what == "MOT":
                    need(dve, ln_done[0], i if live(i - 1) else NG)
                    norm_stats(xn, g, 2, ev["MO"])
                elif what == "LN3":
                    norm_apply(xn, xn, g, 2)

            def mask(i, k):
                got = heads_at(i, k)
                if got is None:
                    return
                kind, g, m = got
                dve.wait_ge(scores[kind], 8 * g + m + 1)
                if kind == "A":
                    dve.wait_ge(bias_r[m], 16 * (g + 1))
                back = heads_before(i, k, 2)
                if back:
                    need(dve, turned[back[0]], 8 * back[1] + back[2] + 1)
                passed(dve, dve_passed)
                for h in range(4):
                    add = bias[m % 3][:, h * T:(h + 1) * T] if kind == "A" else xmask[:, :]
                    nc.vector.tensor_tensor_reduce(prob[k % 2][:, h * T:(h + 1) * T], S[k % 2][:, h * T:(h + 1) * T], add,
                                                   1.0, 3.0e38, ALU.add, ALU.min,
                                                   low[k % 2][:, h:h + 1]).then_inc(masked[kind], 1)

            def invert(i, k):
                got = heads_at(i, k)
                if got is None:
                    return
                kind, g, m = got
                dve.wait_ge(exped[kind], 32 * g + 4 * m + 4)
                nc.vector.reciprocal(inv[k % 2][:, :], total[k % 2][:, :]).then_inc(inved[kind], 1)

            def prob_copy(i, k):
                got = heads_at(i, k)
                if got is None:
                    return
                kind, g, m = got
                dve.wait_ge(turned[kind], 8 * g + m + 1)
                back = heads_before(i, k, 2)
                if back:
                    need(dve, summed[back[0]], 8 * back[1] + back[2] + 1)
                nc.vector.tensor_copy(prob_t[k % 2][:, :], TP[k % 2][:, :]).then_inc(prob_out[kind], 1)

            def one_round(i):
                for k in range(SLOTS):
                    mask(i, k + 1)
                    for it in FILL[k][0]:
                        item(i, *it)
                    prob_copy(i, k)
                    invert(i, k + 1)
                    for it in FILL[k][1]:
                        item(i, *it)

            rounds(dve, one_round)

        @block.gpsimd
        def _(pool):
            nc.gpsimd.memset(c_s[0][:, :], 0.0).then_inc(const_pool, 1)
            nc.gpsimd.memset(c_s[1][:, :], BIG).then_inc(const_pool, 1)
            nc.gpsimd.memset(vx[:, :], 0.0).then_inc(const_pool, 1)
            nc.gpsimd.memset(gate[:, :], 0.0).then_inc(const_pool, 1)
            for j in range(2):
                nc.gpsimd.memset(k_t[j][:, :], 0.0).then_inc(const_pool, 1)
            pool.wait_ge(ld_c[3], 16)
            pool.wait_ge(ld_c[19], 16)
            pool.wait_ge(const_dve, 7)

            def root(g, which):
                pool.wait_ge(stats_ready[which], 2 * g + 2)
                passed(pool, pool_passed)
                r = rstd[which]
                nc.gpsimd.tensor_scalar(r[:, 0:2], mv[:, 1:4:2], EPS, 1.0, ALU.add, ALU.mult).then_inc(eps_added[which], 1)
                pool.wait_ge(eps_added[which], g + 1)
                nc.gpsimd.tensor_tensor(r[:, 2:4], r[:, 0:2], halfpow[:, :], ALU.pow).then_inc(rstd_ready[which], 1)

            def item(i, what, n, off):
                g = i + off
                if not live(g):
                    return
                if what == "XS":
                    pool.wait_ge(x_split, g + 1)
                    nc.gpsimd.tensor_tensor(xt[1][:, :], raw[:, :], xt[0][:, :].bitcast(F32), ALU.subtract).then_inc(x_split_lo, 1)
                elif what == "CS":
                    pool.wait_ge(c_split, g + 1)
                    nc.gpsimd.tensor_tensor(ct[1][:, :], raw[:, :], ct[0][:, :].bitcast(F32), ALU.subtract).then_inc(c_split_lo, 1)
                elif what == "WPT":
                    root(g, 0)
                elif what == "WOT":
                    root(g, 1)
                elif what == "MOT":
                    root(g, 2)
                elif what == "X1C":
                    pool.wait_ge(ln_done[0], g + 1)
                    need(pool, ev["WO"], g)
                    passed(pool, pool_passed)
                    nc.gpsimd.tensor_scalar(x1_old[:, :], x1[:, :], 1.0, 1.0, ALU.mult, ALU.mult).then_inc(x1_kept, 1)
                elif what == "HG":
                    pool.wait_ge(h_hi, 4 * g + n + 1)
                    if n == 1:
                        pool.wait_ge(pe["FC"], 4 * g + 4)
                    need(pool, pe["MO"], 4 * g + n - 1)
                    h = at[:, n * 512:(n + 1) * 512]
                    nc.gpsimd.tensor_tensor(hg_lo[n % 2][:, :], h, hg_hi[n % 3][:, :].bitcast(F32),
                                            ALU.subtract).then_inc(h_lo, 1)

            def normalise(i, k):
                got = heads_at(i, k)
                if got is None:
                    return
                kind, g, m = got
                pool.wait_ge(inved[kind], 8 * g + m + 1)
                p = prob[k % 2][:, :].rearrange("p (h t) -> p h t", h=4)
                nc.gpsimd.tensor_tensor(p, p, inv[k % 2][:, :].unsqueeze(2).to_broadcast([P, 4, T]), ALU.mult).then_inc(normed[kind], 1)

            def one_round(i):
                for k in range(SLOTS):
                    if k == 5 and live(i):
                        pool.wait_ge(ld_xn, 16 * (i + 1))
                        xs = xn[:, :].rearrange("p (s e) -> p s e", s=2)
                        nc.gpsimd.tensor_tensor(xs, xs, bproj_s[:, :].unsqueeze(1).to_broadcast([P, 2, E]), ALU.add).then_inc(xn_ready, 1)
                    for it in FILL[k][0]:
                        item(i, *it)
                    normalise(i, k + 1)
                    for it in FILL[k][1]:
                        item(i, *it)

            rounds(pool, one_round)


def kernel(**inputs):
    import numpy as np
    import concourse.bacc as bacc
    from concourse.bass_utils import run_bass_kernel_spmd

    a = {k: np.asarray(v) for k, v in inputs.items()}
    B, T, E = a["x"].shape
    NE = a["L0_ffn_w_gate"].shape[0]
    nb = a["L0_attn_b_nd"].shape[0]
    tokens_last = lambda v: np.ascontiguousarray(v.reshape(B * T, E).T)
    t = np.arange(P)
    row3 = t // (4 * nb)
    consts = np.zeros((P, 3 * P + 16), np.float32)
    consts[:, 0:P] = np.eye(P)
    consts[:, P:2 * P] = np.where(t[None, :] < P - 1 - t[:, None], BIG, 0.0)
    consts[:, 2 * P:3 * P] = np.where(t[None, :] > t[:, None], BIG, 0.0)
    consts[:, 3 * P + 0] = t % 32 < 16
    consts[:, 3 * P + 1] = t % 32 >= 16
    consts[:, 3 * P + 2] = np.where(row3 == 1, -1.0, 1.0)
    consts[:, 3 * P + 3] = row3 == 1
    consts[:, 3 * P + 4] = np.where(row3 == 2, -1.0, 1.0)
    consts[:, 3 * P + 5] = row3 == 2
    consts[:, 3 * P + 6:3 * P + 8] = -0.5
    consts[:, 3 * P + 8:3 * P + 8 + NE] = np.arange(NE)
    arrays = {
        "x": a["x"], "x_t": tokens_last(a["x"]), "ctx_t": tokens_last(a["ctx_1024"]),
        "wq": a["L0_attn_Wq"], "bq": a["L0_attn_bq"].reshape(-1, P).T, "wk": a["L0_attn_Wk"], "wv": a["L0_attn_Wv"],
        "wproj": a["L0_attn_Wproj"], "bproj": a["L0_attn_bproj"], "wr": a["L0_attn_Wr"], "br": a["L0_attn_br"].reshape(4, -1).T,
        "b_rev": a["L0_attn_b_nd"][:, T - 1::-1],
        "xwq_t": a["L0_xattn_Wq"].T, "xwk_t": a["L0_xattn_Wk"].T, "xwv_t": a["L0_xattn_Wv"].T, "xwo_t": a["L0_xattn_Wo"].T,
        "wg_t": a["L0_ffn_w_gate"].T, "wfc_t": a["L0_ffn_w_fc"].transpose(2, 0, 1), "wpj_t": a["L0_ffn_w_proj"].transpose(2, 0, 1),
        "consts": consts,
    }
    arrays = {k: np.ascontiguousarray(v) for k, v in arrays.items()}
    nc = bacc.Bacc("TRN2", target_bir_lowering=False, num_devices=1)
    aps = {k: nc.dram_tensor(f"in_{k}", v.shape, mybir.dt.from_np(v.dtype), kind="ExternalInput").ap() for k, v in arrays.items()}
    out = nc.dram_tensor("out", (B, T, E), F32, kind="ExternalOutput").ap()
    decoder_kernel(nc, **aps, out=out)
    r = run_bass_kernel_spmd(nc, [{f"in_{k}": v for k, v in arrays.items()}], core_ids=[0])
    return r.results[0]["out"]
```

```python
from contextlib import ExitStack

import concourse.bass as bass
from concourse import mybir

F32 = mybir.dt.float32
F32R = mybir.dt.float32r
U32 = mybir.dt.uint32
ALU = mybir.AluOpType
ACT = mybir.ActivationFunctionType

P = 128
BIG = 1.0e9
EPS = 1e-5

FILL = [
    ([], [("MOT", 0, -3), ("WO", 0, -2)]),
    ([("WON", 0, -2)], [("LN3", 0, -3), ("Q", 2, 0), ("QX", 0, -1), ("WOT", 0, -2)]),
    ([("K", 2, 0), ("LN2", 0, -2)], [("V", 2, 0), ("X2T", 0, -2), ("X2L", 0, -2)]),
    ([("Q", 3, 0)], [("KX", 0, -1), ("RT", 0, -2)]),
    ([("K", 3, 0), ("GX", 0, -2)], [("V", 3, 0), ("XS", 0, 1), ("GA", 0, -2)]),
    ([], [("VX", 0, -1), ("R", 0, 1), ("GATE", 0, -2)]),
    ([("RS", 0, 1), ("Q", 0, 1)], [("K", 0, 1), ("X1C", 0, -1), ("GT", 0, -2)]),
    ([("R", 1, 1)], [("V", 0, 1), ("C", 0, 1), ("RS", 1, 1)]),
    ([("C", 1, 1)], [("WP", 0, 0), ("R", 2, 1), ("C", 2, 1), ("RS", 2, 1)]),
    ([("C", 3, 1)], [("R", 3, 1), ("RS", 3, 1), ("C", 4, 1)]),
    ([("C", 5, 1), ("WP", 1, 0), ("FC", 0, -2)],
     [("FC", 1, -2), ("WPN", 0, 0), ("WPT", 0, 0), ("Q", 1, 1), ("FC", 2, -2), ("FC", 3, -2), ("GB", 0, -2), ("HG", 0, -2)]),
    ([("GB", 1, -2), ("LN1", 0, 0)], [("HG", 1, -2), ("K", 1, 1), ("X1T", 0, 0), ("X1L", 0, 0)]),
    ([("GB", 2, -2)], [("MO", 0, -2), ("C", 6, 1), ("HG", 2, -2)]),
    ([("GB", 3, -2)], [("MO", 1, -2), ("C", 7, 1), ("HG", 3, -2)]),
    ([("V", 1, 1), ("CS", 0, 0)], [("MO", 2, -2)]),
    ([], [("MO", 3, -2), ("MON", 0, -2)]),
]
SLOTS = len(FILL)
BANKED = {"Q": 4, "K": 4, "V": 4, "R": 4, "C": 8, "X1T": 1, "QX": 1, "KX": 1, "VX": 1,
          "WO": 1, "X2T": 1, "RT": 1, "GT": 1, "FC": 4, "GB": 4}
BANK_ORDER = [it for a, b in FILL for it in a + b if it[0] in BANKED]
BANK = {(w, n): j % 2 for j, (w, n, _) in enumerate(BANK_ORDER)}


def decoder_kernel(nc, x, x_t, ctx_t, wq, bq, wk, wv, wproj, bproj, wr, br, b_diag,
                   xwq_t, xwk_t, xwv_t, xwo_t, wg_t, wfc_t, wpj_t, consts, out):
    B, T, E = x.shape
    NG = B // 2
    HD = wq.shape[1]
    H = 16
    DQ = HD // H
    NB = b_diag.shape[0] // 12
    NE, I = wfc_t.shape[1], wfc_t.shape[2]
    XD = E // H
    KC = E // P
    N2 = 2 * T
    LO_ROW = 32
    GR = LO_ROW + NE
    RW = 4 * NB
    R3 = 3 * RW
    ROW = 4 * T + T
    assert T == P and E == 2 * P and DQ == 64 and XD == 16 and I == P and NE == 8 and R3 <= P

    scratch = nc.dram_tensor("bias_scratch", [8, T * ROW], F32, kind="Internal").ap()

    with ExitStack() as es:
        def sb(name, cols, dt=F32, parts=P):
            return es.enter_context(nc.sbuf_tensor(name, [parts, cols], dt))

        def ps(name):
            return es.enter_context(nc.psum_tensor(name, [P, 512], F32))

        def sem(name):
            return es.enter_context(nc.semaphore(name))

        def pair(name, width):
            return sb(name + "_hi", width, F32R), sb(name + "_lo", width, F32R)

        wq_s, wk_s, wv_s = (pair(n, KC * HD) for n in ("wq_s", "wk_s", "wv_s"))
        xwq_s, xwk_s, xwv_s = (pair(n, KC * E) for n in ("xwq_s", "xwk_s", "xwv_s"))
        wr_s = pair("wr_s", KC * 4 * R3)
        wfc_s, wpj_s = pair("wfc_s", KC * NE * I), pair("wpj_s", NE * E)
        wg_s = sb("wg_s", KC * 2 * NE, F32R)
        wp_s = sb("wp_s", (HD // P) * E)
        wo_s = sb("wo_s", KC * E)
        bq_s = sb("bq_s", HD // P)
        br_s = sb("br_s", 4)
        bproj_s = sb("bproj_s", E)
        toep = sb("toep", 4 * T, F32R)
        const = sb("const", consts.shape[1])
        ident, cmask, xmask = const[:, 0:P], const[:, P:2 * P], const[:, 2 * P:3 * P]
        pick, halfpow, iota8 = const[:, 3 * P:3 * P + 6], const[:, 3 * P + 6:3 * P + 8], const[:, 3 * P + 8:3 * P + 16]
        one_r = sb("one_r", NE, F32R, GR)
        raw = sb("raw", KC * N2)
        xt = pair("xt", KC * N2)
        ct = pair("ct", KC * N2)
        qkv = sb("qkv", 2 * 1024)
        q_t, v_s = qkv[:, 0:1024], qkv[:, 1024:2048]
        k_t = [sb(f"k_t{j}", 1024) for j in range(2)]
        at = sb("at", 8 * N2)
        r_st = [sb(f"r_st{j}", N2, F32R) for j in range(2)]
        c_s = [sb(f"c_s{j}", 4 * T) for j in range(2)]
        bias = [sb(f"bias{j}", 4 * T) for j in range(3)]
        prob = [sb(f"prob{j}", 4 * T) for j in range(2)]
        prob_t = [sb(f"prob_t{j}", 4 * T) for j in range(2)]
        low = [sb(f"low{j}", 4) for j in range(2)]
        total = [sb(f"total{j}", 4) for j in range(2)]
        inv = [sb(f"inv{j}", 4) for j in range(2)]
        xn = sb("xn", 2 * E)
        y = sb("y", 2 * E)
        r_f = y[:, 0:N2]
        stat = sb("stat", 2 * 6)
        mv = sb("mv", 2 * 2)
        rstd = [sb(f"rstd{n}", 4) for n in (1, 2, 3)]
        x1 = sb("x1", 2 * E)
        x1_old = sb("x1_old", 2 * E)
        x1_t = pair("x1_t", KC * N2)
        qx = sb("qx", KC * N2)
        kx = [sb(f"kx{j}", KC * N2) for j in range(2)]
        vx = sb("vx", 2 * H * 2 * XD)
        ax = sb("ax", KC * N2)
        x2 = sb("x2", 2 * E)
        x2_t = pair("x2_t", KC * N2)
        logit = sb("logit", 2 * NE)
        top = sb("top", 2 * 8)
        topi = sb("topi", 2 * 8, U32)
        topf = sb("topf", 2 * 8)
        gsc = sb("gsc", 8)
        gate_1, gate_2 = sb("gate_1", 2 * NE), sb("gate_2", 2 * NE)
        gate = sb("gate", 2 * GR)
        g_t = sb("g_t", N2, F32R, GR)
        hg = [sb(f"hg{j}", 2 * N2, F32R) for j in range(3)]
        hg_hi, hg_lo = [hg[0], hg[1], x2_t[0]], [hg[2], x2_t[1]]

        S = [ps("ps_s0"), ps("ps_s1")]
        TP = [ps("ps_t0"), ps("ps_t1")]
        AV = ps("ps_av")
        FB = [ps("ps_f0"), ps("ps_f1")]
        MOB = ps("ps_mo")

        pe = {w: sem(f"pe_{w}") for w in list(BANKED) + ["WP", "MO"]}
        ev = {w: sem(f"ev_{w}") for w in list(BANKED) + ["WP", "MO"]}
        scores = {h: sem(f"scores_{h}") for h in "AB"}
        masked = {h: sem(f"masked_{h}") for h in "AB"}
        exped = {h: sem(f"exped_{h}") for h in "AB"}
        inved = {h: sem(f"inved_{h}") for h in "AB"}
        normed = {h: sem(f"normed_{h}") for h in "AB"}
        turned = {h: sem(f"turned_{h}") for h in "AB"}
        prob_out = {h: sem(f"prob_out_{h}") for h in "AB"}
        summed = {h: sem(f"summed_{h}") for h in "AB"}
        av_out = {h: sem(f"av_out_{h}") for h in "AB"}
        x_split, x_split_lo = sem("x_split"), sem("x_split_lo")
        c_split, c_split_lo = sem("c_split"), sem("c_split_lo")
        r_rounded = sem("r_rounded")
        x1t_hi, x2t_hi = sem("x1t_hi"), sem("x2t_hi")
        xn_ready, x1_kept = sem("xn_ready"), sem("x1_kept")
        stats_ready = [sem(f"stats_ready{n}") for n in (1, 2, 3)]
        rstd_ready = [sem(f"rstd_ready{n}") for n in (1, 2, 3)]
        ln_done = [sem(f"ln_done{n}") for n in (1, 2, 3)]
        tops_ready, gexp_ready, gate_ready = sem("tops_ready"), sem("gexp_ready"), sem("gate_ready")
        gate_copied = sem("gate_copied")
        h_hi, h_lo = sem("h_hi"), sem("h_lo")
        ld_xt, ld_xn, ld_ct, st_out = sem("ld_xt"), sem("ld_xn"), sem("ld_ct"), sem("st_out")
        bias_w = [sem(f"bias_w{k}") for k in range(8)]
        bias_r = [sem(f"bias_r{k}") for k in range(8)]
        ld_w = [sem(f"ld_w{j}") for j in range(4)]
        w_hi, w_lo = sem("w_hi"), sem("w_lo")
        ld_const, ld_br, ld_bq, ld_toep = sem("ld_const"), sem("ld_br"), sem("ld_bq"), sem("ld_toep")
        ld_wp, ld_wo, ld_bproj = sem("ld_wp"), sem("ld_wo"), sem("ld_bproj")
        const_pool, const_dve = sem("const_pool"), sem("const_dve")
        pad_w = sem("pad_w")
        dve_passed, pool_passed, sp_passed, te_passed = (sem(f"{e}_passed") for e in ("dve", "pool", "sp", "te"))
        ev_rs = sem("ev_rs")
        rt_chain, ga_chain = sem("rt_chain"), sem("ga_chain")
        ln_chain = [sem(f"ln_chain{n}") for n in (1, 2, 3)]
        eps_added = [sem(f"eps_added{n}") for n in (1, 2, 3)]

        def live(g):
            return not isinstance(g, int) or 0 <= g < NG

        def need(eng, s, value):
            if not isinstance(value, int) or value > 0:
                eng.wait_ge(s, value)

        def passed(eng, mark):
            eng.sem_inc(mark, 1)

        def heads_at(i, k):
            if k >= SLOTS:
                i, k = i + 1, k - SLOTS
            if k < 0:
                i, k = i - 1, k + SLOTS
            g = i if k < 8 else i - 1
            return ("A" if k < 8 else "B", g, k % 8) if live(g) else None

        def heads_before(i, k, d):
            k -= d
            while True:
                got = heads_at(i, k)
                if got or not isinstance(i, int):
                    return got
                k -= 8
                if 16 * i + k < 0:
                    return None
                while k < 0:
                    i, k = i - 1, k + SLOTS

        def rounds(eng, one_round):
            for i in (-1, 0, 1, 2):
                one_round(i)
            with eng.Fori(3, NG - 1) as i:
                one_round(i)
            for i in (NG - 1, NG, NG + 1, NG + 2):
                one_round(i)

        def chunks(src, halves, cols, factor):
            return [(src[k * P:(k + 1) * P], [t[:, k * cols:(k + 1) * cols] for t in halves], factor) for k in range(KC)]

        def whole(src, halves, cols, factor):
            return [(src.rearrange("(k p) n -> p k n", p=P),
                     [t[:, :].rearrange("p (k n) -> p k n", k=KC) for t in halves], factor)]

        split_w = whole(wr, wr_s, 4 * R3, 1.0)
        split_w += chunks(wq, wq_s, HD, -1.0 / 8.0) + chunks(wk, wk_s, HD, 1.0) + chunks(wv, wv_s, HD, 1.0)
        EARLY = len(split_w)
        split_w += whole(xwq_t, xwq_s, E, -1.0 / 4.0) + whole(xwk_t, xwk_s, E, 1.0) + whole(xwv_t, xwv_s, E, 1.0)
        split_w += [(wg_t.rearrange("(k p) n -> p k n", p=P),
                     [wg_s[:, :].rearrange("p (k d n) -> p k d n", k=KC, d=2)[:, :, d, :] for d in range(2)], 1.0)]
        split_w += chunks(wfc_t.rearrange("p e i -> p (e i)"), wfc_s, NE * I, 1.0)
        split_w += [(wpj_t.rearrange("p e n -> p (e n)")[:, j * 1024:(j + 1) * 1024],
                     [t[:, j * 1024:(j + 1) * 1024] for t in wpj_s], 1.0) for j in range(NE * E // 1024)]
        NW = len(split_w)
        stages = [at[:, 0:1024], at[:, 1024:2048], qkv[:, 0:1024], qkv[:, 1024:2048]]

        def stage_of(n):
            return (0, 1, 2, 3, 0, 1, 0)[n] if n < EARLY else (n - EARLY + 1) % 2

        def stage(n):
            shape = split_w[n][1][0].shape
            cols = shape[1] * (shape[2] if len(shape) == 3 else 1)
            flat = stages[stage_of(n)][:, 0:cols]
            return flat.rearrange("p (k n) -> p k n", k=KC) if len(shape) == 3 else flat

        def loads_before(n):
            return sum(stage_of(j) == stage_of(n) for j in range(n + 1))

        load_slot = {n: 0 if n < EARLY else 6 if n < EARLY + 2 else n - EARLY + 5 for n in range(1, NW)}
        split_slot = {n: 4 + (n - 1) // 2 if n < EARLY else n - EARLY + 7 for n in range(1, NW)}

        x_g = x.rearrange("(g s) t e -> g t s e", s=2)
        out_g = out.rearrange("(g s) t e -> g t s e", s=2)
        xt_g = x_t.rearrange("(k p) (g n) -> g p k n", p=P, n=N2)
        ct_g = ctx_t.rearrange("(k p) (g n) -> g p k n", p=P, n=N2)

        block = es.enter_context(nc.Block())

        @block.sync
        def _(sp):
            def load(n):
                before = [j for j in range(n) if stage_of(j) == stage_of(n)]
                if before:
                    sp.wait_ge(w_lo, before[-1] + 1)
                sp.dma_start(stage(n), split_w[n][0]).then_inc(ld_w[stage_of(n)], 16)

            load(0)
            sp.dma_start(const[:, :], consts[:, :]).then_inc(ld_const, 16)
            sp.dma_start(br_s[0:R3, :], br[:, :]).then_inc(ld_br, 16)
            sp.dma_start(bq_s[:, :], bq[:, :]).then_inc(ld_bq, 16)
            sp.wait_ge(const_pool, 2)
            sp.dma_start(c_s[0][0:R3, :], b_diag[:, :]).then_inc(ld_toep, 16)
            sp.dma_start(scratch[:, :].rearrange("k (t w) -> t k w", w=ROW)[:, :, 4 * T:ROW],
                         c_s[1][:, 0:T].unsqueeze(1).to_broadcast([P, 8, T])).then_inc(pad_w, 16)

            def one_round(i):
                for k in range(SLOTS):
                    if k == 4 and live(i):
                        need(sp, st_out, 16 * (i - 2))
                        sp.dma_start(xn[:, :].rearrange("p (s e) -> p s e", s=2), x_g[i]).then_inc(ld_xn, 16)
                    if k == 0 and live(i + 1):
                        need(sp, c_split, i)
                        need(sp, c_split_lo, i)
                        sp.dma_start(raw[:, :].rearrange("p (k n) -> p k n", k=KC), xt_g[i + 1]).then_inc(ld_xt, 16)
                    if k == 6 and live(i):
                        need(sp, x_split, i + 2 if live(i + 1) else NG)
                        need(sp, x_split_lo, i + 2 if live(i + 1) else NG)
                        sp.dma_start(raw[:, :].rearrange("p (k n) -> p k n", k=KC), ct_g[i]).then_inc(ld_ct, 16)
                    for what, n, off in FILL[k][0] + FILL[k][1]:
                        if what == "C" and live(i + off):
                            need(sp, ev["C"], 8 * (i + off) + n + 1)
                            passed(sp, sp_passed)
                            need(sp, bias_r[n], 16 * (i + off))
                            if isinstance(i, int) and i + off == 0 and n == 0:
                                sp.wait_ge(pad_w, 16)
                            sp.dma_start(scratch[n, :].rearrange("(t w) -> t w", w=ROW)[:, 0:4 * T],
                                         c_s[n % 2][:, :]).then_inc(bias_w[n], 16)
                    if isinstance(i, int) and i == -1:
                        for n in range(1, NW):
                            if load_slot[n] == k:
                                load(n)
                        if k == 0:
                            sp.dma_start(wp_s[:, :].rearrange("p (c n) -> p c n", n=E),
                                         wproj.rearrange("(c p) n -> p c n", p=P)).then_inc(ld_wp, 16)
                            sp.dma_start(wo_s[:, :].rearrange("p (c n) -> p c n", n=E),
                                         xwo_t.rearrange("(c p) n -> p c n", p=P)).then_inc(ld_wo, 16)
                            sp.dma_start(bproj_s[:, :], bproj.rearrange("(a n) -> a n", a=1).to_broadcast([P, E])).then_inc(ld_bproj, 16)
                    g, m = (i, k + 3) if k < 5 else (i + 1, k - 13)
                    if (k < 5 or k >= 13) and live(g):
                        sp.wait_ge(bias_w[m], 16 * (g + 1))
                        passed(sp, sp_passed)
                        need(sp, masked["A"], 32 * g + 4 * (m - 3) + 4 if m >= 3 else 32 * g)
                        sp.dma_start(bias[m % 3][:, :],
                                     scratch[m, T - 1:T - 1 + T * (ROW - 1)].rearrange("(t w) -> t w", w=ROW - 1)[:, 0:4 * T]
                                     ).then_inc(bias_r[m], 16)
                    if k == 2 and live(i - 3):
                        sp.wait_ge(ln_done[2], i - 2)
                        sp.dma_start(out_g[i - 3], xn[:, :].rearrange("p (s e) -> p s e", s=2)).then_inc(st_out, 16)

            rounds(sp, one_round)
            sp.wait_ge(st_out, 16 * NG)

        @block.tensor
        def _(te):
            te.wait_ge(const_dve, 7)
            te.wait_ge(const_pool, 6)
            te.wait_ge(ld_const, 16)
            first_use = {"R": 1, "Q": 3, "K": 5, "V": 7}
            users = [None, None]

            def free_bank(i, what, n):
                b = BANK[(what, n)]
                if users[b] is not None:
                    w, m, g = users[b]
                    need(te, ev[w], BANKED[w] * g + m + 1)
                return FB[b]

            def three(out_ap, stationary, moving, first, last):
                nc.tensor.matmul(out_ap, stationary(0), moving(0), start=first, stop=False)
                nc.tensor.matmul(out_ap, stationary(0), moving(1), start=False, stop=False)
                return nc.tensor.matmul(out_ap, stationary(1), moving(0), start=False, stop=last)

            def cols(t, k, n):
                return t[:, k * n:(k + 1) * n]

            def item(i, what, n, off):
                g = i + off
                if not live(g):
                    return
                if isinstance(i, int) and g == 0 and n == 0:
                    if what in first_use:
                        te.wait_ge(w_lo, first_use[what])
                    elif what == "WP":
                        te.wait_ge(ld_wp, 16)
                    elif what in ("QX", "KX", "VX"):
                        te.wait_ge(w_lo, NW)
                        te.wait_ge(ld_wo, 16)
                if what == "MO":
                    te.wait_ge(h_hi, 4 * g + n + 1)
                    te.wait_ge(h_lo, 4 * g + n + 1)
                    if n == 0:
                        te.wait_ge(ev["WP"], i + 1 if live(i) else NG)
                    h = (hg_hi[n % 3], hg_lo[n % 2])
                    for e in range(2):
                        for s in range(2):
                            for a, b in ((0, 0), (0, 1), (1, 0)):
                                last = nc.tensor.matmul(
                                    MOB[:, s * E:(s + 1) * E], h[a][:, e * N2 + s * T:e * N2 + (s + 1) * T],
                                    cols(wpj_s[b], 2 * n + e, E), start=(n == 0 and e == 0 and s == 0 and a == 0 and b == 0),
                                    stop=(n == 3 and e == 1 and a == 1), skip_group_check=True)
                    last.then_inc(pe["MO"], 1)
                    return
                if what == "WP":
                    te.wait_ge(av_out["A"], 8 * g + 7 + n)
                    if n == 0:
                        need(te, ev["MO"], g - 2)
                    for c in range(8):
                        last = nc.tensor.matmul(MOB[:, n * E:(n + 1) * E], at[:, c * N2 + n * T:c * N2 + (n + 1) * T],
                                                wp_s[:, c * E:(c + 1) * E], start=c == 0, stop=c == 7)
                    if n == 1:
                        last.then_inc(pe["WP"], 1)
                    return
                if what not in BANKED:
                    return
                F = free_bank(i, what, n)
                if what in "QK":
                    if n == 0:
                        te.wait_ge(x_split_lo, g + 1)
                    w = wq_s if what == "Q" else wk_s
                    for j in range(2):
                        c = 2 * n + j
                        for k in range(KC):
                            last = three(F[:, j * N2:(j + 1) * N2],
                                         lambda a: w[a][:, k * HD + c * P:k * HD + (c + 1) * P],
                                         lambda a: cols(xt[a], k, N2), k == 0, k == KC - 1)
                elif what == "V":
                    for s in range(2):
                        for k in range(KC):
                            last = three(F[:, s * 256:(s + 1) * 256],
                                         lambda a: xt[a][:, k * N2 + s * T:k * N2 + (s + 1) * T],
                                         lambda a: wv_s[a][:, k * HD + n * 256:k * HD + (n + 1) * 256], k == 0, k == KC - 1)
                elif what == "R":
                    te.wait_ge(x_split_lo, g + 1)
                    for k in range(KC):
                        last = three(F[0:R3, 0:N2],
                                     lambda a: wr_s[a][:, (k * 4 + n) * R3:(k * 4 + n + 1) * R3],
                                     lambda a: cols(xt[a], k, N2), k == 0, k == KC - 1)
                elif what == "C":
                    hb, s = n // 2, n % 2
                    te.wait_ge(ev_rs, 4 * g + hb + 1)
                    last = nc.tensor.matmul(F[:, :], r_st[hb % 2][0:R3, s * T:(s + 1) * T], toep[0:R3, :],
                                            start=True, stop=True)
                elif what in ("X1T", "X2T"):
                    src, done = (x1, ln_done[0]) if what == "X1T" else (x2, ln_done[1])
                    te.wait_ge(done, g + 1)
                    for k in range(KC):
                        for s in range(2):
                            last = nc.tensor.transpose(F[:, k * N2 + s * T:k * N2 + (s + 1) * T],
                                                       src[:, s * E + k * P:s * E + (k + 1) * P], ident[:, :])
                elif what in ("QX", "KX"):
                    if what == "QX":
                        te.wait_ge(ev["X1T"], g + 1)
                    else:
                        te.wait_ge(c_split_lo, g + 1)
                    w, mov = (xwq_s, x1_t) if what == "QX" else (xwk_s, ct)
                    for c in range(KC):
                        for k in range(KC):
                            last = three(F[:, c * N2:(c + 1) * N2],
                                         lambda a: w[a][:, k * E + c * P:k * E + (c + 1) * P],
                                         lambda a: cols(mov[a], k, N2), k == 0, k == KC - 1)
                elif what == "VX":
                    te.wait_ge(c_split_lo, g + 1)
                    for s in range(2):
                        for k in range(KC):
                            last = three(F[:, s * E:(s + 1) * E],
                                         lambda a: ct[a][:, k * N2 + s * T:k * N2 + (s + 1) * T],
                                         lambda a: cols(xwv_s[a], k, E), k == 0, k == KC - 1)
                elif what == "WO":
                    te.wait_ge(av_out["B"], 8 * g + 8)
                    for s in range(2):
                        for c in range(KC):
                            last = nc.tensor.matmul(F[:, s * E:(s + 1) * E], ax[:, c * N2 + s * T:c * N2 + (s + 1) * T],
                                                    cols(wo_s, c, E), start=c == 0, stop=c == KC - 1)
                elif what == "RT":
                    te.wait_ge(ev["X2T"], g + 1)
                    for s in range(2):
                        for k in range(KC):
                            nc.tensor.matmul(F[:, 2 * s * NE:2 * (s + 1) * NE], x2_t[0][:, k * N2 + s * T:k * N2 + (s + 1) * T],
                                             wg_s[:, 2 * k * NE:2 * (k + 1) * NE], start=k == 0, stop=False,
                                             skip_group_check=True)
                            last = nc.tensor.matmul(F[:, 2 * s * NE:(2 * s + 1) * NE],
                                                    x2_t[1][:, k * N2 + s * T:k * N2 + (s + 1) * T],
                                                    wg_s[:, 2 * k * NE:(2 * k + 1) * NE], start=False, stop=k == KC - 1,
                                                    skip_group_check=True)
                elif what == "GT":
                    te.wait_ge(gate_ready, 2 * g + 2)
                    passed(te, te_passed)
                    for s in range(2):
                        last = nc.tensor.transpose(F[0:GR, s * T:(s + 1) * T], gate[:, s * GR:(s + 1) * GR], ident[:, :])
                elif what == "GB":
                    te.wait_ge(ev["GT"], g + 1)
                    for e in range(2):
                        last = nc.tensor.matmul(F[:, e * N2:(e + 1) * N2],
                                                one_r[:, 2 * n + e:2 * n + e + 1].to_broadcast([GR, P]), g_t[:, :],
                                                start=True, stop=True)
                elif what == "FC":
                    for e in range(2):
                        for k in range(KC):
                            last = three(F[:, e * N2:(e + 1) * N2],
                                         lambda a: wfc_s[a][:, k * NE * I + (2 * n + e) * I:k * NE * I + (2 * n + e + 1) * I],
                                         lambda a: cols(x2_t[a], k, N2), k == 0, k == KC - 1)
                last.then_inc(pe[what], 1)
                users[BANK[(what, n)]] = (what, n, g)

            def score(i, k):
                got = heads_at(i, k)
                if got is None:
                    return
                kind, g, m = got
                hb, s = m // 2, m % 2
                back = heads_before(i, k, 2)
                if back:
                    need(te, masked[back[0]], 32 * back[1] + 4 * back[2] + 4)
                if kind == "A":
                    te.wait_ge(ev["Q"], 4 * g + hb + 1)
                    te.wait_ge(ev["K"], 4 * g + hb + 1)
                else:
                    te.wait_ge(ev["QX"], g + 1)
                    te.wait_ge(ev["KX"], g + 1)
                for h in range(4):
                    if kind == "A":
                        col = (hb % 2) * 512 + (h // 2) * N2 + s * T
                        lhs, rhs = q_t[:, col:col + T], k_t[h % 2][:, col:col + T]
                    else:
                        r = 32 * hb
                        col = (h // 2) * N2 + s * T
                        lhs, rhs = qx[r:r + 32, col:col + T], kx[h % 2][r:r + 32, col:col + T]
                    last = nc.tensor.matmul(S[k % 2][:, h * T:(h + 1) * T], lhs, rhs, start=True, stop=True)
                last.then_inc(scores[kind], 1)

            def turn(i, k):
                got = heads_at(i, k)
                if got is None:
                    return
                kind, g, m = got
                te.wait_ge(normed[kind], 8 * g + m + 1)
                back = heads_before(i, k, 2)
                if back:
                    need(te, prob_out[back[0]], 8 * back[1] + back[2] + 1)
                for h in range(4):
                    last = nc.tensor.transpose(TP[k % 2][:, h * T:(h + 1) * T], prob[k % 2][:, h * T:(h + 1) * T], ident[:, :])
                last.then_inc(turned[kind], 1)

            def weigh(i, k):
                got = heads_at(i, k)
                if got is None:
                    return
                kind, g, m = got
                hb, s = m // 2, m % 2
                te.wait_ge(prob_out[kind], 8 * g + m + 1)
                back = heads_before(i, k, 1)
                if back:
                    need(te, av_out[back[0]], 8 * back[1] + back[2] + 1)
                if kind == "A":
                    te.wait_ge(ev["V"], 4 * g + hb + 1)
                else:
                    te.wait_ge(ev["VX"], g + 1)
                for h in range(4):
                    rhs = prob_t[k % 2][:, h * T:(h + 1) * T]
                    if kind == "A":
                        col = (hb % 2) * 512 + s * 256 + h * DQ
                        last = nc.tensor.matmul(AV[64 * (h % 2):64 * (h % 2) + 64, (h // 2) * T:(h // 2 + 1) * T],
                                                v_s[:, col:col + DQ], rhs, start=True, stop=True)
                    else:
                        c = h // 2
                        col = s * H * 32 + (8 * c + 2 * hb + h % 2) * 32
                        last = nc.tensor.matmul(AV[32 * hb:32 * hb + 32, c * T:(c + 1) * T], vx[:, col:col + 32], rhs,
                                                start=h % 2 == 0, stop=h % 2 == 1)
                last.then_inc(summed[kind], 1)

            def one_round(i):
                if not isinstance(i, int):
                    for what, n, off in BANK_ORDER[-2:]:
                        users[BANK[(what, n)]] = (what, n, i - 1 + off)
                for k in range(SLOTS):
                    score(i, k + 1)
                    for it in FILL[k][0]:
                        item(i, *it)
                    turn(i, k)
                    for it in FILL[k][1]:
                        item(i, *it)
                    weigh(i, k)
                if not isinstance(i, int):
                    for what, n, off in BANK_ORDER[-2:]:
                        users[BANK[(what, n)]] = (what, n, NG - 2 + off)

            rounds(te, one_round)

        @block.scalar
        def _(act):
            def split_high(n):
                _, (high, _), f = split_w[n]
                act.wait_ge(ld_w[stage_of(n)], 16 * loads_before(n))
                nc.scalar.activation(high, stage(n), ACT.Copy, scale=f).then_inc(w_hi, 1)

            split_high(0)
            act.wait_ge(const_dve, 7)
            act.wait_ge(ld_br, 16)
            act.wait_ge(const_pool, 6)

            def item(i, what, n, off):
                g = i + off
                if not live(g):
                    return
                F = FB[BANK[(what, n)]] if what in BANKED else None
                if what == "Q":
                    act.wait_ge(pe["Q"], 4 * g + n + 1)
                    need(act, scores["A"], 8 * g + 2 * (n - 2) + 2)
                    if isinstance(i, int) and g == 0 and n == 0:
                        act.wait_ge(w_lo, 4)
                    for j in range(2):
                        last = nc.scalar.activation(q_t[:, (n % 2) * 512 + j * N2:(n % 2) * 512 + (j + 1) * N2],
                                                    F[:, j * N2:(j + 1) * N2], ACT.Identity,
                                                    bias=bq_s[:, 2 * n + j:2 * n + j + 1])
                    last.then_inc(ev["Q"], 1)
                elif what == "K":
                    act.wait_ge(pe["K"], 4 * g + n + 1)
                    need(act, scores["A"], 8 * g + 2 * (n - 2) + 2)
                    for j in range(2):
                        last = nc.scalar.activation(k_t[j][64 * j:64 * j + 64, (n % 2) * 512:(n % 2 + 1) * 512],
                                                    F[64 * j:64 * j + 64, :], ACT.Copy)
                    last.then_inc(ev["K"], 1)
                elif what == "V":
                    act.wait_ge(pe["V"], 4 * g + n + 1)
                    need(act, summed["A"], 8 * g + 2 * (n - 2) + 2)
                    nc.scalar.activation(v_s[:, (n % 2) * 512:(n % 2 + 1) * 512], F[:, :], ACT.Copy).then_inc(ev["V"], 1)
                elif what == "R":
                    act.wait_ge(pe["R"], 4 * g + n + 1)
                    need(act, ev_rs, 4 * g + n)
                    nc.scalar.activation(r_f[0:R3, :], F[0:R3, 0:N2], ACT.Identity,
                                         bias=br_s[0:R3, n:n + 1]).then_inc(ev["R"], 1)
                elif what in ("X1T", "X2T"):
                    t, s, last = (x1_t, x1t_hi, pe["QX"]) if what == "X1T" else (x2_t, x2t_hi, pe["FC"])
                    act.wait_ge(pe[what], g + 1)
                    need(act, last, g if what == "X1T" else 4 * g)
                    nc.scalar.activation(t[0][:, :], F[:, :], ACT.Copy).then_inc(s, 1)
                elif what == "QX":
                    act.wait_ge(pe["QX"], g + 1)
                    need(act, scores["B"], 8 * g)
                    nc.scalar.activation(qx[:, :], F[:, :], ACT.Copy).then_inc(ev["QX"], 1)
                elif what == "GX":
                    act.wait_ge(tops_ready, g + 1)
                    nc.scalar.activation(gsc[:, 2:4], gsc[:, 0:2], ACT.Exp).then_inc(gexp_ready, 1)
                elif what == "FC":
                    act.wait_ge(pe["FC"], 4 * g + n + 1)
                    need(act, pe["WP"], (i + 1) if live(i) else NG)
                    nc.scalar.activation(at[:, n * 512:(n + 1) * 512], F[:, :], ACT.Gelu).then_inc(ev["FC"], 1)

            def exps(i, k):
                got = heads_at(i, k)
                if got is None:
                    return
                kind, g, m = got
                p = prob[k % 2]
                for h in range(4):
                    act.wait_ge(masked[kind], 32 * g + 4 * m + h + 1)
                    nc.scalar.activation(p[:, h * T:(h + 1) * T], p[:, h * T:(h + 1) * T], ACT.Exp,
                                         bias=low[k % 2][:, h:h + 1], scale=-1.0,
                                         accum_out=total[k % 2][:, h:h + 1]).then_inc(exped[kind], 1)

            def av(i, k):
                got = heads_at(i, k)
                if got is None:
                    return
                kind, g, m = got
                hb, s = m // 2, m % 2
                act.wait_ge(summed[kind], 8 * g + m + 1)
                if kind == "A":
                    if m == 0:
                        need(act, pe["WP"], g)
                        if isinstance(i, int) and i == 0:
                            act.wait_ge(w_lo, NW)
                        need(act, h_lo, 4 * (g - 2))
                    dst = at[:, :].rearrange("p (c s t) -> p c s t", c=8, s=2)[:, 2 * hb:2 * hb + 2, s, :]
                    nc.scalar.activation(dst, AV[:, 0:2 * T].rearrange("p (c t) -> p c t", c=2), ACT.Copy).then_inc(av_out["A"], 1)
                else:
                    if m == 0:
                        need(act, pe["WO"], g)
                    r = 32 * hb
                    dst = ax[r:r + 32, :].rearrange("p (c s t) -> p c s t", c=2, s=2)[:, :, s, :]
                    nc.scalar.activation(dst, AV[r:r + 32, 0:2 * T].rearrange("p (c t) -> p c t", c=2), ACT.Copy).then_inc(av_out["B"], 1)

            def one_round(i):
                for k in range(SLOTS):
                    exps(i, k + 1)
                    for it in FILL[k][0] + FILL[k][1]:
                        item(i, *it)
                    av(i, k)
                    if isinstance(i, int) and i == -1:
                        for n in range(1, NW):
                            if split_slot[n] == k:
                                split_high(n)

            rounds(act, one_round)

        @block.vector
        def _(dve):
            def split_low(n):
                _, (high, low_part), f = split_w[n]
                dve.wait_ge(w_hi, n + 1)
                nc.vector.scalar_tensor_tensor(out=low_part, in0=stage(n), scalar=f, in1=high.bitcast(F32), op0=ALU.mult,
                                               op1=ALU.subtract).then_inc(w_lo, 1)

            split_low(0)
            dve.wait_ge(ld_bq, 16)
            nc.vector.tensor_scalar(bq_s[:, :], bq_s[:, :], -1.0 / 8.0, None, ALU.mult).then_inc(const_dve, 1)
            dve.wait_ge(ld_toep, 16)
            dve.wait_ge(ld_const, 16)
            nc.vector.tensor_scalar(c_s[0][0:R3, :], c_s[0][0:R3, :], -1.0, None, ALU.mult).then_inc(const_dve, 1)
            dve.wait_ge(const_dve, 2)
            nc.vector.tensor_copy(toep[0:R3, :], c_s[0][0:R3, :]).then_inc(const_dve, 1)
            dve.wait_ge(const_dve, 3)
            nc.vector.tensor_scalar(y[0:R3, :], toep[0:R3, :].bitcast(F32), pick[0:R3, 4:5], None, ALU.mult).then_inc(const_dve, 1)
            dve.wait_ge(const_dve, 4)
            nc.vector.scalar_tensor_tensor(out=toep[0:R3, :], in0=c_s[0][0:R3, :], scalar=pick[0:R3, 5:6], in1=y[0:R3, :],
                                           op0=ALU.mult, op1=ALU.add).then_inc(const_dve, 1)
            nc.vector.tensor_copy(one_r[0:LO_ROW, :], ident[0:LO_ROW, 0:NE]).then_inc(const_dve, 1)
            nc.vector.tensor_copy(one_r[LO_ROW:GR, :], ident[LO_ROW:GR, LO_ROW:GR]).then_inc(const_dve, 1)
            dve.wait_ge(const_dve, 7)
            dve.wait_ge(pad_w, 16)
            dve.wait_ge(const_pool, 6)

            def norm_sum(dst, F, res, n_sem):
                nc.vector.tensor_tensor(dst[:, :], F, res, ALU.add).then_inc(n_sem, 1)

            def norm_stats(src, g, which, n_sem):
                ch = ln_chain[which]
                dve.wait_ge(n_sem, g + 1)
                for s in range(2):
                    nc.vector.bn_stats(stat[:, 6 * s:6 * s + 6], src[:, s * E:(s + 1) * E]).then_inc(ch, 1)
                dve.wait_ge(ch, 2 * g + 2)
                passed(dve, dve_passed)
                for s in range(2):
                    nc.vector.bn_aggr(mv[:, 2 * s:2 * s + 2], stat[:, 6 * s:6 * s + 6]).then_inc(stats_ready[which], 1)

            def norm_apply(dst, src, g, which):
                dve.wait_ge(rstd_ready[which], g + 1)
                for s in range(2):
                    last = nc.vector.tensor_scalar(dst[:, s * E:(s + 1) * E], src[:, s * E:(s + 1) * E],
                                                   mv[:, 2 * s:2 * s + 1], rstd[which][:, 2 + s:3 + s], ALU.subtract, ALU.mult)
                last.then_inc(ln_done[which], 1)

            def item(i, what, n, off):
                g = i + off
                if not live(g):
                    return
                F = FB[BANK[(what, n)]] if what in BANKED else None
                if what == "XS":
                    dve.wait_ge(ld_xt, 16 * (g + 1))
                    need(dve, pe["V"], 4 * g)
                    nc.vector.tensor_copy(xt[0][:, :], raw[:, :]).then_inc(x_split, 1)
                elif what == "CS":
                    dve.wait_ge(ld_ct, 16 * (g + 1))
                    need(dve, pe["VX"], g)
                    nc.vector.tensor_copy(ct[0][:, :], raw[:, :]).then_inc(c_split, 1)
                elif what == "RS":
                    dve.wait_ge(ev["R"], 4 * g + n + 1)
                    need(dve, pe["C"], 8 * g + 2 * (n - 2) + 2)
                    r = r_st[n % 2][0:R3, :]
                    nc.vector.tensor_scalar(r, r_f[0:R3, :], pick[0:R3, 2:3], None, ALU.mult).then_inc(r_rounded, 1)
                    dve.wait_ge(r_rounded, 4 * g + n + 1)
                    nc.vector.scalar_tensor_tensor(out=r, in0=r_f[0:R3, :], scalar=pick[0:R3, 3:4], in1=r.bitcast(F32),
                                                   op0=ALU.mult, op1=ALU.add).then_inc(ev_rs, 1)
                elif what == "C":
                    dve.wait_ge(pe["C"], 8 * g + n + 1)
                    if n >= 2:
                        dve.wait_ge(bias_w[n - 2], 16 * (g + 1))
                    else:
                        need(dve, bias_w[n + 6], 16 * g)
                    nc.vector.tensor_tensor(c_s[n % 2][:, :].rearrange("p (h t) -> p h t", h=4),
                                            F[:, :].rearrange("p (h t) -> p h t", h=4),
                                            cmask[:, :].unsqueeze(1).to_broadcast([P, 4, T]), ALU.add).then_inc(ev["C"], 1)
                elif what == "WPN":
                    dve.wait_ge(pe["WP"], g + 1)
                    dve.wait_ge(xn_ready, g + 1)
                    need(dve, ln_done[1], g - 1)
                    need(dve, ev_rs, 4 * (i + 2 if live(i + 1) else NG))
                    norm_sum(y, MOB[:, :], xn[:, :], ev["WP"])
                elif what == "WPT":
                    norm_stats(y, g, 0, ev["WP"])
                elif what == "LN1":
                    need(dve, x1_kept, g)
                    need(dve, pe["X1T"], g)
                    norm_apply(x1, y, g, 0)
                elif what in ("X1L", "X2L"):
                    w, t, s = ("X1T", x1_t, x1t_hi) if what == "X1L" else ("X2T", x2_t, x2t_hi)
                    dve.wait_ge(s, g + 1)
                    nc.vector.tensor_tensor(t[1][:, :], FB[BANK[(w, 0)]][:, :], t[0][:, :].bitcast(F32),
                                            ALU.subtract).then_inc(ev[w], 1)
                elif what == "KX":
                    dve.wait_ge(pe["KX"], g + 1)
                    need(dve, scores["B"], 8 * g)
                    for j in range(2):
                        last = nc.vector.tensor_scalar(kx[j][:, :], F[:, :], pick[:, j:j + 1], None, ALU.mult)
                    last.then_inc(ev["KX"], 1)
                elif what == "VX":
                    dve.wait_ge(pe["VX"], g + 1)
                    need(dve, summed["B"], 8 * g)
                    for s in range(2):
                        dst = vx[:, s * 512:(s + 1) * 512].rearrange("p (h a d) -> p h a d", a=4, d=XD)[:, :, 0:4:3, :]
                        last = nc.vector.tensor_copy(dst, F[:, s * E:(s + 1) * E].rearrange("p (h a d) -> p h a d", a=2, d=XD))
                    last.then_inc(ev["VX"], 1)
                elif what == "WON":
                    dve.wait_ge(pe["WO"], g + 1)
                    dve.wait_ge(x1_kept, g + 1)
                    need(dve, ln_done[0], i if live(i - 1) else NG)
                    norm_sum(y, FB[BANK[("WO", 0)]][:, :], x1_old[:, :], ev["WO"])
                elif what == "WOT":
                    need(dve, ln_done[2], g)
                    norm_stats(y, g, 1, ev["WO"])
                elif what == "LN2":
                    need(dve, ev["MO"], g)
                    norm_apply(x2, y, g, 1)
                elif what == "RT":
                    dve.wait_ge(pe["RT"], g + 1)
                    parts = F[:, 0:4 * NE].rearrange("p (s d n) -> p s d n", s=2, d=2)
                    nc.vector.tensor_reduce(logit[:, :].rearrange("p (s n) -> p s n", s=2), parts.rearrange("p s d n -> p s n d"),
                                            mybir.AxisListType.X, ALU.add).then_inc(ev["RT"], 1)
                    dve.wait_ge(ev["RT"], g + 1)
                    passed(dve, dve_passed)
                    for s in range(2):
                        nc.vector.max(top[:, 8 * s:8 * s + 8], logit[:, NE * s:NE * s + NE]).then_inc(rt_chain, 1)
                    dve.wait_ge(rt_chain, 5 * g + 2)
                    passed(dve, dve_passed)
                    for s in range(2):
                        nc.vector.max_index(topi[:, 8 * s:8 * s + 8], top[:, 8 * s:8 * s + 8],
                                            logit[:, NE * s:NE * s + NE]).then_inc(rt_chain, 1)
                    dve.wait_ge(rt_chain, 5 * g + 4)
                    nc.vector.tensor_copy(topf[:, :], topi[:, :]).then_inc(rt_chain, 1)
                    ranked = top[:, :].rearrange("p (s j) -> p s j", s=2)
                    nc.vector.tensor_tensor(gsc[:, 0:2].unsqueeze(2), ranked[:, :, 1:2], ranked[:, :, 0:1],
                                            ALU.subtract).then_inc(tops_ready, 1)
                elif what == "GA":
                    dve.wait_ge(gexp_ready, g + 1)
                    dve.wait_ge(rt_chain, 5 * g + 5)
                    nc.vector.tensor_scalar(gsc[:, 4:6], gsc[:, 2:4], 1.0, None, ALU.add).then_inc(ga_chain, 1)
                    dve.wait_ge(ga_chain, 7 * g + 1)
                    nc.vector.reciprocal(gsc[:, 4:6], gsc[:, 4:6]).then_inc(ga_chain, 1)
                    dve.wait_ge(ga_chain, 7 * g + 2)
                    nc.vector.tensor_tensor(gsc[:, 2:4], gsc[:, 2:4], gsc[:, 4:6], ALU.mult).then_inc(ga_chain, 1)
                elif what == "GATE":
                    dve.wait_ge(ga_chain, 7 * g + 3)
                    for t, rank, at_rank in ((gate_1, 0, 4), (gate_2, 1, 2)):
                        for s in range(2):
                            nc.vector.tensor_scalar(t[:, NE * s:NE * s + NE], iota8[:, :], topf[:, 8 * s + rank:8 * s + rank + 1],
                                                    gsc[:, at_rank + s:at_rank + s + 1], ALU.is_equal,
                                                    ALU.mult).then_inc(ga_chain, 1)
                    need(dve, pe["GT"], g)
                    dve.wait_ge(ga_chain, 7 * g + 7)
                    for d in (0, LO_ROW):
                        nc.vector.tensor_tensor(gate[:, :].rearrange("p (s n) -> p s n", s=2)[:, :, d:d + NE],
                                                gate_1[:, :].rearrange("p (s n) -> p s n", s=2),
                                                gate_2[:, :].rearrange("p (s n) -> p s n", s=2), ALU.add).then_inc(gate_ready, 1)
                elif what == "GT":
                    dve.wait_ge(pe["GT"], g + 1)
                    need(dve, pe["GB"], 4 * g)
                    nc.vector.tensor_copy(g_t[:, :], F[0:GR, 0:N2]).then_inc(gate_copied, 1)
                    dve.wait_ge(gate_copied, g + 1)
                    nc.vector.tensor_tensor(g_t[LO_ROW:GR, :], F[LO_ROW:GR, 0:N2], g_t[LO_ROW:GR, :].bitcast(F32),
                                            ALU.subtract).then_inc(ev["GT"], 1)
                elif what == "GB":
                    dve.wait_ge(pe["GB"], 4 * g + n + 1)
                    dve.wait_ge(ev["FC"], 4 * g + n + 1)
                    h = at[:, n * 512:(n + 1) * 512]
                    nc.vector.tensor_tensor(h, h, F[:, :], ALU.mult).then_inc(ev["GB"], 1)
                elif what == "HG":
                    dve.wait_ge(ev["GB"], 4 * g + n + 1)
                    if n == 2:
                        dve.wait_ge(pe["FC"], 4 * g + 4)
                    need(dve, pe["MO"], 4 * g + n - 2)
                    h = at[:, n * 512:(n + 1) * 512]
                    nc.vector.tensor_copy(hg_hi[n % 3][:, :], h).then_inc(h_hi, 1)
                elif what == "MON":
                    dve.wait_ge(pe["MO"], 4 * g + 4)
                    dve.wait_ge(ev["WP"], i + 1 if live(i) else NG)
                    if not live(i):
                        dve.wait_ge(st_out, 16 * g)
                    norm_sum(xn, MOB[:, :], x2[:, :], ev["MO"])
                elif what == "MOT":
                    need(dve, ln_done[0], i if live(i - 1) else NG)
                    norm_stats(xn, g, 2, ev["MO"])
                elif what == "LN3":
                    norm_apply(xn, xn, g, 2)

            def mask(i, k):
                got = heads_at(i, k)
                if got is None:
                    return
                kind, g, m = got
                dve.wait_ge(scores[kind], 8 * g + m + 1)
                if kind == "A":
                    dve.wait_ge(bias_r[m], 16 * (g + 1))
                back = heads_before(i, k, 2)
                if back:
                    need(dve, turned[back[0]], 8 * back[1] + back[2] + 1)
                passed(dve, dve_passed)
                for h in range(4):
                    add = bias[m % 3][:, h * T:(h + 1) * T] if kind == "A" else xmask[:, :]
                    nc.vector.tensor_tensor_reduce(prob[k % 2][:, h * T:(h + 1) * T], S[k % 2][:, h * T:(h + 1) * T], add,
                                                   1.0, 3.0e38, ALU.add, ALU.min,
                                                   low[k % 2][:, h:h + 1]).then_inc(masked[kind], 1)

            def invert(i, k):
                got = heads_at(i, k)
                if got is None:
                    return
                kind, g, m = got
                dve.wait_ge(exped[kind], 32 * g + 4 * m + 4)
                nc.vector.reciprocal(inv[k % 2][:, :], total[k % 2][:, :]).then_inc(inved[kind], 1)

            def prob_copy(i, k):
                got = heads_at(i, k)
                if got is None:
                    return
                kind, g, m = got
                dve.wait_ge(turned[kind], 8 * g + m + 1)
                back = heads_before(i, k, 2)
                if back:
                    need(dve, summed[back[0]], 8 * back[1] + back[2] + 1)
                nc.vector.tensor_copy(prob_t[k % 2][:, :], TP[k % 2][:, :]).then_inc(prob_out[kind], 1)

            def one_round(i):
                for k in range(SLOTS):
                    mask(i, k + 1)
                    for it in FILL[k][0]:
                        item(i, *it)
                    prob_copy(i, k)
                    invert(i, k + 1)
                    for it in FILL[k][1]:
                        item(i, *it)
                    if isinstance(i, int) and i == -1:
                        for n in range(1, NW):
                            if split_slot[n] == k:
                                split_low(n)

            rounds(dve, one_round)

        @block.gpsimd
        def _(pool):
            nc.gpsimd.memset(c_s[0][:, :], 0.0).then_inc(const_pool, 1)
            nc.gpsimd.memset(c_s[1][:, :], BIG).then_inc(const_pool, 1)
            nc.gpsimd.memset(vx[:, :], 0.0).then_inc(const_pool, 1)
            nc.gpsimd.memset(gate[:, :], 0.0).then_inc(const_pool, 1)
            for j in range(2):
                nc.gpsimd.memset(k_t[j][:, :], 0.0).then_inc(const_pool, 1)
            pool.wait_ge(ld_const, 16)
            pool.wait_ge(const_dve, 7)

            def root(g, which):
                pool.wait_ge(stats_ready[which], 2 * g + 2)
                passed(pool, pool_passed)
                r = rstd[which]
                nc.gpsimd.tensor_scalar(r[:, 0:2], mv[:, 1:4:2], EPS, 1.0, ALU.add, ALU.mult).then_inc(eps_added[which], 1)
                pool.wait_ge(eps_added[which], g + 1)
                nc.gpsimd.tensor_tensor(r[:, 2:4], r[:, 0:2], halfpow[:, :], ALU.pow).then_inc(rstd_ready[which], 1)

            def item(i, what, n, off):
                g = i + off
                if not live(g):
                    return
                if what == "XS":
                    pool.wait_ge(x_split, g + 1)
                    nc.gpsimd.tensor_tensor(xt[1][:, :], raw[:, :], xt[0][:, :].bitcast(F32), ALU.subtract).then_inc(x_split_lo, 1)
                elif what == "CS":
                    pool.wait_ge(c_split, g + 1)
                    nc.gpsimd.tensor_tensor(ct[1][:, :], raw[:, :], ct[0][:, :].bitcast(F32), ALU.subtract).then_inc(c_split_lo, 1)
                elif what == "WPT":
                    root(g, 0)
                elif what == "WOT":
                    root(g, 1)
                elif what == "MOT":
                    root(g, 2)
                elif what == "X1C":
                    pool.wait_ge(ln_done[0], g + 1)
                    need(pool, ev["WO"], g)
                    passed(pool, pool_passed)
                    nc.gpsimd.tensor_scalar(x1_old[:, :], x1[:, :], 1.0, 1.0, ALU.mult, ALU.mult).then_inc(x1_kept, 1)
                elif what == "HG":
                    pool.wait_ge(h_hi, 4 * g + n + 1)
                    if n == 1:
                        pool.wait_ge(pe["FC"], 4 * g + 4)
                    need(pool, pe["MO"], 4 * g + n - 1)
                    h = at[:, n * 512:(n + 1) * 512]
                    nc.gpsimd.tensor_tensor(hg_lo[n % 2][:, :], h, hg_hi[n % 3][:, :].bitcast(F32),
                                            ALU.subtract).then_inc(h_lo, 1)

            def normalise(i, k):
                got = heads_at(i, k)
                if got is None:
                    return
                kind, g, m = got
                pool.wait_ge(inved[kind], 8 * g + m + 1)
                p = prob[k % 2][:, :].rearrange("p (h t) -> p h t", h=4)
                nc.gpsimd.tensor_tensor(p, p, inv[k % 2][:, :].unsqueeze(2).to_broadcast([P, 4, T]), ALU.mult).then_inc(normed[kind], 1)

            def one_round(i):
                for k in range(SLOTS):
                    if k == 5 and live(i):
                        if isinstance(i, int) and i == 0:
                            pool.wait_ge(ld_bproj, 16)
                        pool.wait_ge(ld_xn, 16 * (i + 1))
                        xs = xn[:, :].rearrange("p (s e) -> p s e", s=2)
                        nc.gpsimd.tensor_tensor(xs, xs, bproj_s[:, :].unsqueeze(1).to_broadcast([P, 2, E]), ALU.add).then_inc(xn_ready, 1)
                    for it in FILL[k][0]:
                        item(i, *it)
                    normalise(i, k + 1)
                    for it in FILL[k][1]:
                        item(i, *it)

            rounds(pool, one_round)


def kernel(**inputs):
    import numpy as np
    import concourse.bacc as bacc
    from concourse.bass_utils import run_bass_kernel_spmd

    a = {k: np.asarray(v) for k, v in inputs.items()}
    B, T, E = a["x"].shape
    NE = a["L0_ffn_w_gate"].shape[0]
    nb = a["L0_attn_b_nd"].shape[0]
    tokens_last = lambda v: np.ascontiguousarray(v.reshape(B * T, E).T)
    t = np.arange(P)
    row3 = t // (4 * nb)
    consts = np.zeros((P, 3 * P + 16), np.float32)
    consts[:, 0:P] = np.eye(P)
    consts[:, P:2 * P] = np.where(t[None, :] < P - 1 - t[:, None], BIG, 0.0)
    consts[:, 2 * P:3 * P] = np.where(t[None, :] > t[:, None], BIG, 0.0)
    consts[:, 3 * P + 0] = t % 32 < 16
    consts[:, 3 * P + 1] = t % 32 >= 16
    consts[:, 3 * P + 2] = np.where(row3 == 1, -1.0, 1.0)
    consts[:, 3 * P + 3] = row3 == 1
    consts[:, 3 * P + 4] = np.where(row3 == 2, -1.0, 1.0)
    consts[:, 3 * P + 5] = row3 == 2
    consts[:, 3 * P + 6:3 * P + 8] = -0.5
    consts[:, 3 * P + 8:3 * P + 8 + NE] = np.arange(NE)
    thrice = lambda w: np.tile(w.reshape(w.shape[0], 4, 1, -1), (1, 1, 3, 1)).reshape(w.shape[0], -1)
    b_diag = np.zeros((3, 4, nb, 4, T), np.float32)
    for h in range(4):
        b_diag[:, h, :, h, :] = a["L0_attn_b_nd"][:, T - 1::-1]
    b_diag = b_diag.reshape(12 * nb, 4 * T)
    arrays = {
        "x": a["x"], "x_t": tokens_last(a["x"]), "ctx_t": tokens_last(a["ctx_1024"]),
        "wq": a["L0_attn_Wq"], "bq": a["L0_attn_bq"].reshape(-1, P).T, "wk": a["L0_attn_Wk"], "wv": a["L0_attn_Wv"],
        "wproj": a["L0_attn_Wproj"], "bproj": a["L0_attn_bproj"], "wr": thrice(a["L0_attn_Wr"]), "br": thrice(a["L0_attn_br"][None])[0].reshape(4, -1).T,
        "b_diag": b_diag,
        "xwq_t": a["L0_xattn_Wq"].T, "xwk_t": a["L0_xattn_Wk"].T, "xwv_t": a["L0_xattn_Wv"].T, "xwo_t": a["L0_xattn_Wo"].T,
        "wg_t": a["L0_ffn_w_gate"].T, "wfc_t": a["L0_ffn_w_fc"].transpose(2, 0, 1), "wpj_t": a["L0_ffn_w_proj"].transpose(2, 0, 1),
        "consts": consts,
    }
    arrays = {k: np.ascontiguousarray(v) for k, v in arrays.items()}
    nc = bacc.Bacc("TRN2", target_bir_lowering=False, num_devices=1)
    aps = {k: nc.dram_tensor(f"in_{k}", v.shape, mybir.dt.from_np(v.dtype), kind="ExternalInput").ap() for k, v in arrays.items()}
    out = nc.dram_tensor("out", (B, T, E), F32, kind="ExternalOutput").ap()
    decoder_kernel(nc, **aps, out=out)
    r = run_bass_kernel_spmd(nc, [{f"in_{k}": v for k, v in arrays.items()}], core_ids=[0])
    return r.results[0]["out"]
```
